# Optimizing a Trainium2 kernel written in Bass

```python
import numpy as np
import jax
import jax.numpy as jnp

def _softmax(x, axis=-1):
    return jax.nn.softmax(x, axis=axis)

def _gelu(x):
    return jax.nn.gelu(x, approximate=True)

def _silu(x):
    return jax.nn.silu(x)

def _sigmoid(x):
    return jax.nn.sigmoid(x)

def _layernorm(x, axis=-1, eps=1e-05):
    m = jnp.mean(x, axis=axis, keepdims=True)
    v = jnp.var(x, axis=axis, keepdims=True)
    return (x - m) / jnp.sqrt(v + eps)

def _scatter_add(tgt, idx, src, axis=0):
    return tgt.at[idx].add(src)

def _segment_sum(src, seg, n):
    return jax.ops.segment_sum(src, seg, n)
kernel_name = 'mk_seq_preln_d1_jaxref_r8_71cda4'

def setup_inputs(seed: int=0):
    np.random.seed(seed)
    _w = jnp.asarray

    def _L0_attn_setup():
        import jax, jax.numpy as jnp
        import numpy as np
        N_EMBD = 128
        QK_DIM = 16
        key = jax.random.key(seed)
        k1, k2, k3, k4, k5 = jax.random.split(key, 5)
        b, s = (8, 256)
        lim = 1.0 / np.sqrt(N_EMBD)
        return {'x': jax.random.normal(k1, (b, s, N_EMBD), dtype=jnp.float32), 'w_q': jax.random.uniform(k2, (QK_DIM, N_EMBD), minval=-lim, maxval=lim, dtype=jnp.float32), 'b_q': jax.random.uniform(k3, (QK_DIM,), minval=-lim, maxval=lim, dtype=jnp.float32), 'w_k': jax.random.uniform(k4, (QK_DIM, N_EMBD), minval=-lim, maxval=lim, dtype=jnp.float32), 'b_k': jax.random.uniform(k5, (QK_DIM,), minval=-lim, maxval=lim, dtype=jnp.float32)}
    _L0_attn_in = _L0_attn_setup()

    def _L0_ffn_setup():
        import jax, jax.numpy as jnp
        import numpy as np
        DIM = 128
        DEPTH = 6
        HEADS = 16
        DIM_HEAD = 64
        WINDOW = 32
        INNER = HEADS * DIM_HEAD
        DIM_INNER = int(DIM * 4 * 2 / 3)
        QK_SCALE = 8.0

        def shift_tokens(t):
            a, s = jnp.split(t, 2, -1)
            s = jnp.pad(s, ((0, 0), (1, 0), (0, 0)))[:, :-1]
            return jnp.concatenate([a, s], -1)

        def l2norm(t):
            return t / jnp.maximum(jnp.linalg.norm(t, axis=-1, keepdims=True), 1e-12)

        def rotate_half(x):
            x1, x2 = jnp.split(x, 2, -1)
            return jnp.concatenate([-x2, x1], -1)

        def rotary_tables(n):
            half = jnp.arange(0, DIM_HEAD, 2, dtype=jnp.float32)
            inv_freq = 1.0 / 10000.0 ** (half / DIM_HEAD)
            t = jnp.arange(n, dtype=jnp.float32)
            freqs = t[:, None] * inv_freq[None, :]
            freqs = jnp.concatenate([freqs, freqs], -1)
            base_scale = (half + 0.4 * DIM_HEAD) / (1.4 * DIM_HEAD)
            power = (t - n // 2) / (WINDOW // 2)
            scale = base_scale[None, :] ** power[:, None]
            scale = jnp.concatenate([scale, scale], -1)
            return (freqs, scale)

        def local_attention(q, k, v):
            b, h, n, d = q.shape
            w = WINDOW
            nw = n // w
            bq = q.reshape(b, h, nw, w, d)
            bk = k.reshape(b, h, nw, w, d)
            bv = v.reshape(b, h, nw, w, d)

            def look(t):
                p = jnp.pad(t, ((0, 0), (0, 0), (1, 0), (0, 0), (0, 0)))
                return jnp.concatenate([p[:, :, :nw], p[:, :, 1:]], axis=3)
            bk2, bv2 = (look(bk), look(bv))
            seq = jnp.arange(n).reshape(nw, w)
            seq_p = jnp.pad(seq, ((1, 0), (0, 0)), constant_values=-1)
            jt = jnp.concatenate([seq_p[:nw], seq_p[1:]], axis=1)
            it = seq[:, :, None]
            jb = jt[:, None, :]
            mask = (it < jb) | (it > jb + w) | (jb == -1)
            sim = jnp.einsum('bhwie,bhwje->bhwij', bq, bk2) * QK_SCALE
            sim = jnp.where(mask, -jnp.finfo(sim.dtype).max, sim)
            attn = jax.nn.softmax(sim, -1)
            out = jnp.einsum('bhwij,bhwje->bhwie', attn, bv2)
            return out.reshape(b, h, n, d)

        def attn_layer(x, Wqkv, qs, ksc, Wo):
            b, n, _ = x.shape
            qkv = x @ Wqkv
            q, k, v = jnp.split(qkv, 3, -1)
            sh = lambda t: t.reshape(b, n, HEADS, DIM_HEAD).transpose(0, 2, 1, 3)
            q, k, v = (sh(q), sh(k), sh(v))
            q = l2norm(q) * qs
            k = l2norm(k) * ksc
            freqs, scale = rotary_tables(n)
            cos, sin = (jnp.cos(freqs), jnp.sin(freqs))
            q = q * cos * scale + rotate_half(q) * sin * scale
            inv = 1.0 / scale
            k = k * cos * inv + rotate_half(k) * sin * inv
            out = local_attention(q, k, v)
            out = out.transpose(0, 2, 1, 3).reshape(b, n, INNER)
            return out @ Wo

        def ffn_layer(x, g, bln, W1, b1, W2, b2):
            mu = x.mean(-1, keepdims=True)
            var = ((x - mu) ** 2).mean(-1, keepdims=True)
            xn = (x - mu) / jnp.sqrt(var + 1e-05) * g + bln
            hg = xn @ W1 + b1
            a, gate = jnp.split(hg, 2, -1)
            return a * jax.nn.gelu(gate, approximate=False) @ W2 + b2
        key = jax.random.key(seed)
        ks = jax.random.split(key, 8)
        B, N = (2, 256)
        init = lambda k, shape: jax.random.normal(k, shape, jnp.float32) * 0.02
        return {'x': jax.random.normal(ks[0], (B, N, DIM), jnp.float32), 'Wqkv': init(ks[1], (DEPTH, DIM, 3 * INNER)), 'q_scale': jnp.ones((DEPTH, DIM_HEAD), jnp.float32), 'k_scale': jnp.ones((DEPTH, DIM_HEAD), jnp.float32), 'Wo': init(ks[2], (DEPTH, INNER, DIM)), 'ln_g': jnp.ones((DEPTH, DIM), jnp.float32), 'ln_b': jnp.zeros((DEPTH, DIM), jnp.float32), 'W1': init(ks[3], (DEPTH, DIM, 2 * DIM_INNER)), 'b1': jnp.zeros((DEPTH, 2 * DIM_INNER), jnp.float32), 'W2': init(ks[4], (DEPTH, DIM_INNER, DIM)), 'b2': jnp.zeros((DEPTH, DIM), jnp.float32)}
    _L0_ffn_in = _L0_ffn_setup()
    _d = {'L0_attn_x': _L0_attn_in['x'], 'L0_attn_w_q': _L0_attn_in['w_q'], 'L0_attn_b_q': _L0_attn_in['b_q'], 'L0_attn_w_k': _L0_attn_in['w_k'], 'L0_attn_b_k': _L0_attn_in['b_k'], 'L0_ffn_Wqkv': _L0_ffn_in['Wqkv'], 'L0_ffn_q_scale': _L0_ffn_in['q_scale'], 'L0_ffn_k_scale': _L0_ffn_in['k_scale'], 'L0_ffn_Wo': _L0_ffn_in['Wo'], 'L0_ffn_ln_g': _L0_ffn_in['ln_g'], 'L0_ffn_ln_b': _L0_ffn_in['ln_b'], 'L0_ffn_W1': _L0_ffn_in['W1'], 'L0_ffn_b1': _L0_ffn_in['b1'], 'L0_ffn_W2': _L0_ffn_in['W2'], 'L0_ffn_b2': _L0_ffn_in['b2']}
    _x0 = _d['L0_attn_x']
    _d['L0_attn_x'] = jax.random.normal(jax.random.fold_in(jax.random.key(seed), 1), (16, 256, 128), dtype=_x0.dtype)
    del _x0
    return _d

def reference(L0_attn_x, L0_attn_w_q, L0_attn_b_q, L0_attn_w_k, L0_attn_b_k, L0_ffn_Wqkv, L0_ffn_q_scale, L0_ffn_k_scale, L0_ffn_Wo, L0_ffn_ln_g, L0_ffn_ln_b, L0_ffn_W1, L0_ffn_b1, L0_ffn_W2, L0_ffn_b2):

    def _L0_attn_ref(x, w_q, b_q, w_k, b_k):
        import jax, jax.numpy as jnp
        import numpy as np
        N_EMBD = 128
        QK_DIM = 16
        s = x.shape[-2]
        q = jnp.einsum('bsd,ed->bse', x, w_q) + b_q
        k = jnp.einsum('bsd,ed->bse', x, w_k) + b_k
        scale = 1.0 / jnp.sqrt(jnp.asarray(QK_DIM, dtype=x.dtype))
        mask = jnp.arange(s)[:, None] >= jnp.arange(s)[None, :]
        scores = jnp.einsum('bqe,bke->bqk', q, k) * scale
        scores = jnp.where(mask[None], scores, jnp.asarray(-10000.0, dtype=x.dtype))
        probs = jax.nn.softmax(scores, axis=-1)
        return jnp.einsum('bqk,bkv->bqv', probs, x)

    def _L0_ffn_ref(x, Wqkv, q_scale, k_scale, Wo, ln_g, ln_b, W1, b1, W2, b2):
        import jax, jax.numpy as jnp
        import numpy as np
        DIM = 128
        DEPTH = 6
        HEADS = 16
        DIM_HEAD = 64
        WINDOW = 32
        INNER = HEADS * DIM_HEAD
        DIM_INNER = int(DIM * 4 * 2 / 3)
        QK_SCALE = 8.0

        def shift_tokens(t):
            a, s = jnp.split(t, 2, -1)
            s = jnp.pad(s, ((0, 0), (1, 0), (0, 0)))[:, :-1]
            return jnp.concatenate([a, s], -1)

        def l2norm(t):
            return t / jnp.maximum(jnp.linalg.norm(t, axis=-1, keepdims=True), 1e-12)

        def rotate_half(x):
            x1, x2 = jnp.split(x, 2, -1)
            return jnp.concatenate([-x2, x1], -1)

        def rotary_tables(n):
            half = jnp.arange(0, DIM_HEAD, 2, dtype=jnp.float32)
            inv_freq = 1.0 / 10000.0 ** (half / DIM_HEAD)
            t = jnp.arange(n, dtype=jnp.float32)
            freqs = t[:, None] * inv_freq[None, :]
            freqs = jnp.concatenate([freqs, freqs], -1)
            base_scale = (half + 0.4 * DIM_HEAD) / (1.4 * DIM_HEAD)
            power = (t - n // 2) / (WINDOW // 2)
            scale = base_scale[None, :] ** power[:, None]
            scale = jnp.concatenate([scale, scale], -1)
            return (freqs, scale)

        def local_attention(q, k, v):
            b, h, n, d = q.shape
            w = WINDOW
            nw = n // w
            bq = q.reshape(b, h, nw, w, d)
            bk = k.reshape(b, h, nw, w, d)
            bv = v.reshape(b, h, nw, w, d)

            def look(t):
                p = jnp.pad(t, ((0, 0), (0, 0), (1, 0), (0, 0), (0, 0)))
                return jnp.concatenate([p[:, :, :nw], p[:, :, 1:]], axis=3)
            bk2, bv2 = (look(bk), look(bv))
            seq = jnp.arange(n).reshape(nw, w)
            seq_p = jnp.pad(seq, ((1, 0), (0, 0)), constant_values=-1)
            jt = jnp.concatenate([seq_p[:nw], seq_p[1:]], axis=1)
            it = seq[:, :, None]
            jb = jt[:, None, :]
            mask = (it < jb) | (it > jb + w) | (jb == -1)
            sim = jnp.einsum('bhwie,bhwje->bhwij', bq, bk2) * QK_SCALE
            sim = jnp.where(mask, -jnp.finfo(sim.dtype).max, sim)
            attn = jax.nn.softmax(sim, -1)
            out = jnp.einsum('bhwij,bhwje->bhwie', attn, bv2)
            return out.reshape(b, h, n, d)

        def attn_layer(x, Wqkv, qs, ksc, Wo):
            b, n, _ = x.shape
            qkv = x @ Wqkv
            q, k, v = jnp.split(qkv, 3, -1)
            sh = lambda t: t.reshape(b, n, HEADS, DIM_HEAD).transpose(0, 2, 1, 3)
            q, k, v = (sh(q), sh(k), sh(v))
            q = l2norm(q) * qs
            k = l2norm(k) * ksc
            freqs, scale = rotary_tables(n)
            cos, sin = (jnp.cos(freqs), jnp.sin(freqs))
            q = q * cos * scale + rotate_half(q) * sin * scale
            inv = 1.0 / scale
            k = k * cos * inv + rotate_half(k) * sin * inv
            out = local_attention(q, k, v)
            out = out.transpose(0, 2, 1, 3).reshape(b, n, INNER)
            return out @ Wo

        def ffn_layer(x, g, bln, W1, b1, W2, b2):
            mu = x.mean(-1, keepdims=True)
            var = ((x - mu) ** 2).mean(-1, keepdims=True)
            xn = (x - mu) / jnp.sqrt(var + 1e-05) * g + bln
            hg = xn @ W1 + b1
            a, gate = jnp.split(hg, 2, -1)
            return a * jax.nn.gelu(gate, approximate=False) @ W2 + b2
        for i in range(DEPTH):
            x = attn_layer(shift_tokens(x), Wqkv[i], q_scale[i], k_scale[i], Wo[i]) + x
            x = ffn_layer(shift_tokens(x), ln_g[i], ln_b[i], W1[i], b1[i], W2[i], b2[i]) + x
        return x
    x = L0_attn_x
    x = x + _L0_attn_ref(_layernorm(x, axis=-1), L0_attn_w_q, L0_attn_b_q, L0_attn_w_k, L0_attn_b_k)
    x = x + _L0_ffn_ref(_layernorm(x, axis=-1), L0_ffn_Wqkv, L0_ffn_q_scale, L0_ffn_k_scale, L0_ffn_Wo, L0_ffn_ln_g, L0_ffn_ln_b, L0_ffn_W1, L0_ffn_b1, L0_ffn_W2, L0_ffn_b2)
    return x

_drawn_inputs = setup_inputs


def setup_inputs(seed=0):
    import zlib

    import numpy as np

    out = dict(_drawn_inputs(seed))
    spreads = {'L0_ffn_q_scale': (1.0, 0.6),
     'L0_ffn_k_scale': (1.0, 0.6),
     'L0_ffn_ln_g': (1.0, 0.6),
     'L0_ffn_ln_b': (0.0, 0.8),
     'L0_ffn_b1': (0.0, 0.8),
     'L0_ffn_b2': (0.0, 0.1)}
    factors = {'L0_attn_b_q': 8.0, 'L0_attn_b_k': 8.0, 'L0_ffn_W1': 3.701, 'L0_ffn_W2': 3.63}
    for name, (base, spread) in spreads.items():
        noise = np.random.default_rng([zlib.crc32(name.encode()), seed]).standard_normal(out[name].shape)
        drawn = base * np.exp(spread * noise) if base else spread * noise
        out[name] = jnp.asarray(drawn.astype(out[name].dtype))
    for name, factor in factors.items():
        out[name] = (out[name] * factor).astype(out[name].dtype)
    return out
```

```python
from contextlib import ExitStack

import numpy as np
import concourse.bass as bass
from concourse import mybir

F32 = mybir.dt.float32
F32R = mybir.dt.float32r
BF16 = mybir.dt.bfloat16
I32 = mybir.dt.int32
ALU = mybir.AluOpType
ACT = mybir.ActivationFunctionType
AX = mybir.AxisListType

B, S, D = 16, 256, 128
E = 16
DEPTH, HEADS, DH, WIN = 6, 16, 64, 32
INNER = HEADS * DH
NW = S // WIN
HALF = DH // 2
HPG = 4
G = HEADS // HPG
FF = int(D * 4 * 2 / 3)
FCH = [min(128, FF - c * 128) for c in range((FF + 127) // 128)]
NT = B * S // 128
TPB = S // 128
RING = 2 * G
CLOCKS = DEPTH * B * G
PAIRS = B // 2
LAG_R, LAG_S, LAG_T, LAG_PV = 5, 6, 7, 8
LAG_F = 4
FU = 8
NEWTON = 14
ROOT = 15
MAGIC = float(0x5F3759DF)
LN_EPS = 1e-5
MASKED = -1e30
SEL = 32 - HPG + 96
ORDER = [0, 2, 1, 3, 4, 6, 5, 7]
NEG = -10000.0


def constants():
    c = {}
    c["ident"] = np.eye(128, dtype=np.float32)
    p = np.arange(128)
    at = np.arange(SEL)[None] - (32 - HPG)
    c["sel"] = ((at >= 0) & (at % 32 == p[:, None] // HALF)).astype(np.float32)
    c["mean"] = np.full((128, 128), 1.0 / D, np.float32)
    row = np.arange(96)[:, None, None] % 32
    c["spread"] = (row == (HPG * np.arange(2 * G)[None, :, None] + p[None, None, :] // HALF)).astype(np.float32)
    a, b = (p % WIN)[:, None], np.arange(WIN)[None]
    prev = np.where(a > b, MASKED, 0.0)
    own = np.where(a < b, MASKED, 0.0)
    m = np.zeros((128, NW, 2, WIN))
    m[:, :, 0] = prev[:, None]
    m[:, 0, 0] = MASKED
    m[:, :, 1] = own[:, None]
    m = m[:, ORDER]
    c["wmask"] = m.reshape(128, NW * 2 * WIN).astype(np.float32)
    half = np.arange(0, DH, 2, dtype=np.float32)
    inv_freq = (1.0 / 10000.0 ** (half / DH)).astype(np.float32)
    t = np.arange(S, dtype=np.float32)
    freqs = (t[:, None] * inv_freq[None, :]).astype(np.float32)
    base = ((half + 0.4 * DH) / (1.4 * DH)).astype(np.float32)
    scale = (base[None, :] ** ((t - S // 2) / (WIN // 2))[:, None]).astype(np.float32)
    cos, sin = np.cos(freqs), np.sin(freqs)
    tabs = [cos * scale * 8.0, sin * scale * 8.0, cos * (1 / scale), sin * (1 / scale)]
    c["rot"] = np.stack([np.tile(x.T, (HPG, 1)) for x in tabs], 1).astype(np.float32)
    q = (p[:, None] + 128 * np.arange(TPB)[None])[:, :, None]
    seen = q >= np.arange(S)[None, None]
    c["cmask"] = np.stack([np.where(seen, 0.25, 0.0), np.where(seen, 0.0, NEG)], 1).astype(np.float32)
    return c


CONST_NAMES = ["ident", "sel", "mean", "wmask", "rot", "cmask"]


def live(m):
    return not isinstance(m, int) or 0 <= m < CLOCKS


def wait(eng, sem, value):
    if isinstance(value, int) and value <= 0:
        return
    eng.wait_ge(sem, value)


def wait_apart(eng, sem, value, settled):
    if isinstance(value, int) and value <= 0:
        return
    if not isinstance(value, int):
        value = eng.to_reg(value)
    eng.wait_ge(settled, 1)
    eng.wait_ge(sem, value)


def schedule(eng, body, reload_projection, reload_rest):
    body(0, 0, 0, None)
    body(RING, 2, 1, None)
    with eng.Fori(0, DEPTH - 1) as layer:
        n_layer, i_layer = layer * (PAIRS * RING), layer * B
        with eng.Fori(2, PAIRS) as p:
            body(n_layer + p * RING, i_layer + p * 2, p, p - 2)
        reload_projection(layer)
        with eng.Fori(0, 2) as p:
            body(n_layer + p * RING + PAIRS * RING, i_layer + p * 2 + B, p, p + (PAIRS - 2))
        reload_rest(layer)
    n_last = (DEPTH - 1) * PAIRS * RING
    with eng.Fori(2, PAIRS) as p:
        body(p * RING + n_last, p * 2 + (DEPTH - 1) * B, p, p - 2)
    body(CLOCKS, DEPTH * B, None, PAIRS - 2)
    body(CLOCKS + RING, DEPTH * B + 2, None, PAIRS - 1)


def build(nc, a, out):
    with ExitStack() as ctx:
        def sb(name, shape, dt=F32):
            return ctx.enter_context(nc.sbuf_tensor(name, shape, dt))

        def sem(name):
            return ctx.enter_context(nc.semaphore(name))

        ps = [ctx.enter_context(nc.psum_tensor(f"bank{i}", [128, 512], F32)) for i in range(8)]
        p_qk, p_v, p_t, p_s, p_o, p_rb = ps[0:2], ps[2], ps[3], ps[4], ps[5:7], ps[7]
        x1_dram = nc.dram_tensor("x1_scratch", [128, NT, D], F32, kind="Internal").ap()

        X = sb("X", [128, B, S + 1])
        raw = sb("raw", [128, 3 * INNER])
        qk_hi = sb("qk_hi", [128, G, 2, 2, 128], F32R)
        qk_lo = sb("qk_lo", [128, G, 2, 2, 128], F32R)
        v_hi = sb("v_hi", [128, G, 256], F32R)
        v_lo = sb("v_lo", [128, G, 256], F32R)
        wo = sb("wo", [128, 2 * G, D])
        w1_hi = sb("w1_hi", [128, len(FCH), 2, 128], F32R)
        w1_lo = sb("w1_lo", [128, len(FCH), 2, 128], F32R)
        w2 = sb("w2", [128, len(FCH), D])
        rot = sb("rot", [128, 4, S])
        tab = sb("tab", [128, 2, 2, 2, S])
        xs_hi = sb("xs_hi", [128, 2, WIN + S], F32R)
        xs_lo = sb("xs_lo", [128, 2, WIN + S], F32R)
        turned = sb("turned", [128, 2, S])
        squares = sb("squares", [128, 2, 2, S])
        rotated = sb("rotated", [128, RING, 2, 2, S])
        qr = sb("qr", [128, 2, S])
        qbd = sb("qbd", [128, 2, 2, NW, HPG, WIN])
        probs = sb("probs", [128, 2, NW, 2 * WIN])
        pt = sb("pt", [128, 4, 128])
        vring = sb("vring", [128, RING, 4, 256])
        ot = sb("ot", [128, RING, 2, S])
        f_xs = sb("f_xs", [128, S])
        f_xc = sb("f_xc", [128, S])
        f_sq = sb("f_sq", [128, S])
        f_hi = sb("f_hi", [128, S], F32R)
        f_lo = sb("f_lo", [128, S], F32R)
        hid = sb("hid", [128, len(FCH), S])
        wmask = sb("wmask", [128, 512], BF16)
        ident = sb("ident", [128, 128])
        ident_b = sb("ident_b", [128, 128], BF16)
        sel = sb("sel", [128, SEL])
        mean = sb("mean", [128, 128])
        norm = sb("norm", [96, S])
        nt_y = sb("nt_y", [96, S])
        nt_t = sb("nt_t", [96, S])
        r_rows = sb("r_rows", [96, S], BF16)
        r_sel = sb("r_sel", [96, 2 * G, 128], BF16)
        lv = sb("lv", [128, 3, TPB])
        rl_parts = sb("rl_parts", [128, 3, TPB], BF16)
        top = sb("top", [128, NW])
        total = sb("total", [128, 2, NW])
        vecs_all = sb("vecs_all", [128, DEPTH, 9])
        vecs = sb("vecs", [128, 9])
        qks_all = sb("qks_all", [128, DEPTH, 4])
        qks = sb("qks", [128, 4])

        def flat(t, pattern):
            return t[:].rearrange(pattern)
        rot_flat = flat(rotated, "p a b c d -> p (a b c d)")
        x_tok = rot_flat[:, 0:NT * D].rearrange("p (t d) -> p t d", d=D)
        xc_tok = rot_flat[:, NT * D:2 * NT * D].rearrange("p (t d) -> p t d", d=D)
        v_flat = flat(vring, "p a b c -> p (a b c)")
        sq_tok = v_flat[:, 0:NT * D].rearrange("p (t d) -> p t d", d=D)
        x1_back = sq_tok
        cmask = v_flat[:, NT * D:NT * D + 4 * S].rearrange("p (a t k) -> p a t k", a=2, t=TPB)
        ot_flat = flat(ot, "p a b c -> p (a b c)")
        xl = ot_flat[:, 0:256].rearrange("p (t d) -> p t d", d=D)
        xl_t = ot_flat[:, 256:512]
        qk_a = ot_flat[0:E, 512:1024].rearrange("p (s t) -> p s t", s=2)
        sc = ot_flat[:, 1024:1536].rearrange("p (t k) -> p t k", t=TPB)
        pt_a = ot_flat[:, 1536:2048].rearrange("p (k q) -> p k q", k=TPB)
        x_fin = ot_flat[:, 2048:2304]
        st = ot_flat[:, 2304:2432].rearrange("p (k t) -> p k t", k=4)
        wqk_t = ot_flat[:, 2432:2464].rearrange("p (s e) -> p s e", s=2)
        bqk = ot_flat[0:E, 2464:2466]
        amx, asum, arec = (ot_flat[:, 2466 + TPB * k:2468 + TPB * k] for k in range(3))
        r_sel_f = raw[0:96, 0:2 * G * 128].rearrange("p (a x) -> p a x", a=2 * G)
        wmask_f = hid[:].rearrange("p a b -> p (a b)")[:, 0:512]
        w1_raw = hid[:].rearrange("p a b -> p (a b)")[:, 0:2 * FF]

        names = """loads wload rest_load wo_load cload x_load x1_saved x1_loaded out_done
            xs_ready qk_done rot_done sq_done added v_done v_out n_done n_copied newton  r_done r_used
            spread s_done top_done centred exp_done summed total_done scaled t_done t_out pv_done o_out
            f_done f_free fx_ready fsq_ready fc_ready lnewton  fn_ready fn_hi fn_lo gelu_done
            hi_ready lo_ready w1hi_ready w1lo_ready tab_ready vec_ready zeroed consts stats a_dve a_step
            a_xl a_tr a_trc a_qk a_qkc a_sc a_masked a_max a_exp a_rec a_ptr a_ptc a_av a_x1 y_tr y_out
            sq_summed fin_copy fin_tr fin_add pool_zero mask_ready one_step m_step""".split()
        q = {n: sem(n) for n in names}
        W = type("Sems", (), q)

        rb = p_rb[:]
        rb2 = rb.rearrange("p (s t) -> p s t", s=2)
        rbb = rb.bitcast(BF16)

        block = ctx.enter_context(nc.Block())

        @block.sync
        def _(sp):
            for c in range(4):
                sp.dma_start(x_tok[:, 8 * c:8 * c + 8, :],
                             a["L0_attn_x"].rearrange("b (t p) d -> p (b t) d", p=128)[:, 8 * c:8 * c + 8, :]
                             ).then_inc(W.x_load, 16)
            sp.dma_start(ident[:], a["ident"]).then_inc(W.cload, 16)
            sp.dma_start(sel[:], a["sel"]).then_inc(W.cload, 16)
            sp.dma_start(mean[:], a["mean"]).then_inc(W.cload, 16)
            sp.dma_start(r_sel_f, a["spread"]).then_inc(W.cload, 16)
            sp.dma_start(wmask_f, a["wmask"]).then_inc(W.cload, 16)
            sp.dma_start(rot[:], a["rot"]).then_inc(W.cload, 16)
            sp.dma_start(cmask, a["cmask"]).then_inc(W.cload, 16)
            sp.dma_start(wqk_t, a["wqk_t"]).then_inc(W.cload, 16)
            sp.dma_start(bqk, a["bqk"]).then_inc(W.cload, 16)
            sp.dma_start(qks_all[:], a["qks"]).then_inc(W.cload, 16)
            sp.dma_start(vecs_all[:], a["vecs"]).then_inc(W.cload, 16)
            def load_rest(layer):
                sp.dma_start(w1_raw, a["L0_ffn_W1"][layer]).then_inc(W.rest_load, 16)
                sp.dma_start(w2[:, 0:2, :], a["L0_ffn_W2"][layer, 0:256, :].rearrange("(c p) d -> p c d", p=128)
                             ).then_inc(W.rest_load, 16)
                sp.dma_start(w2[0:FCH[2], 2, :], a["L0_ffn_W2"][layer, 256:FF, :]).then_inc(W.rest_load, 16)

            def load_wo(layer):
                sp.dma_start(wo[:], a["L0_ffn_Wo"][layer].rearrange("(c p) d -> p c d", p=128)
                             ).then_inc(W.wo_load, 16)

            load_wo(0)
            sp.wait_ge(W.mask_ready, 2)
            sp.dma_start(raw[:], a["L0_ffn_Wqkv"][0]).then_inc(W.wload, 16)
            load_rest(0)
            sp.wait_ge(W.a_x1, 2 * B)
            sp.dma_start(x1_dram, x_tok).then_inc(W.x1_saved, 16)
            sp.wait_ge(W.lo_ready, G)
            sp.dma_start(raw[:], a["L0_ffn_Wqkv"][1]).then_inc(W.wload, 16)
            sp.wait_ge(W.zeroed, 1)

            def clocks(n0, lo_c, hi_c):
                for c in range(lo_c, hi_c):
                    m = n0 + c - LAG_R
                    if not live(m):
                        continue
                    wait_apart(sp, W.r_used, m * 2 + 1, W.zeroed)
                    wait_apart(sp, W.s_done, m - 1, W.zeroed)
                    wait_apart(sp, W.spread, m * 64, W.zeroed)
                    for j in range(HPG):
                        rows = slice(HALF * j, HALF * (j + 1))
                        sp.dma_start(qbd[rows, c % 2, :, :, j, :],
                                     qr[rows, :, :].rearrange("p x (w t) -> p x w t", w=NW)).then_inc(W.spread, 16)

            clocks(0, 0, RING)
            clocks(RING, 0, RING)
            with sp.Fori(0, DEPTH - 1) as layer:
                nl, il = layer * (PAIRS * RING), layer * B
                with sp.Fori(2, PAIRS) as p:
                    clocks(nl + p * RING, 0, RING)
                for j in range(2):
                    n0 = nl + (PAIRS + j) * RING
                    if j == 0:
                        clocks(n0, 0, RING)
                        continue
                    clocks(n0, 0, 6)
                    wait_apart(sp, W.f_done, (il + (B - 1)) * FU + 1, W.zeroed)
                    load_wo(layer + 1)
                    clocks(n0, 6, RING)
                wait_apart(sp, W.f_free, (il + B) * FU + 1, W.zeroed)
                load_rest(layer + 1)
                wait_apart(sp, W.lo_ready, (layer + 2) * G, W.zeroed)
                nxt = (layer + 2) % DEPTH
                sp.dma_start(raw[:], a["L0_ffn_Wqkv"][nxt]).then_inc(W.wload, 16)
            with sp.Fori(2, PAIRS) as p:
                clocks(p * RING + (DEPTH - 1) * PAIRS * RING, 0, RING)
            clocks(CLOCKS, 0, RING)
            sp.wait_ge(W.pv_done, 2 * CLOCKS)
            sp.wait_ge(W.x1_saved, 16)
            sp.dma_start(x1_back, x1_dram).then_inc(W.x1_loaded, 16)
            out_v = out.rearrange("b (t p) d -> p b t d", p=128)
            with sp.Fori(0, B) as b:
                wait_apart(sp, W.fin_add, b + 1 + 1, W.zeroed)
                sp.dma_start(out_v[:, b, :, :], x1_back.rearrange("p (b t) d -> p b t d", t=TPB)[:, b, :, :]
                             ).then_inc(W.out_done, 16)
            sp.wait_ge(W.wload, 16 * (DEPTH + 1))
            sp.wait_ge(W.out_done, 16 * B)

        @block.tensor
        def _(pe):
            mm = nc.tensor.matmul

            def split3(dst, w_hi, w_lo, x_hi, x_lo):
                mm(dst, w_lo, x_hi, start=True, stop=False)
                mm(dst, w_hi, x_lo, start=False, stop=False)
                return mm(dst, w_hi, x_hi, start=False, stop=True)

            pe.wait_ge(W.cload, 16 * CLOADS)
            with pe.Fori(0, B) as b:
                pe.wait_ge(W.a_xl, b + 1)
                for t in range(TPB):
                    ins = nc.tensor.transpose(ps[0][:, 128 * t:128 * t + 128], xl[:, t, :], ident[:])
                ins.then_inc(W.a_tr, 1)
                pe.wait_ge(W.a_trc, b + 1)
                for s in range(2):
                    ins = mm(ps[1][0:E, 256 * s:256 * s + 256], wqk_t[:, s, :], xl_t, start=True, stop=True)
                ins.then_inc(W.a_qk, 1)
                pe.wait_ge(W.a_qkc, 2 * b + 2)
                for t in range(TPB):
                    ins = mm(ps[2][:, 256 * t:256 * t + 256], qk_a[:, 0, 128 * t:128 * t + 128], qk_a[:, 1, :],
                             start=True, stop=True)
                ins.then_inc(W.a_sc, 1)
                pe.wait_ge(W.a_exp, 2 * b + 2)
                for k in range(TPB):
                    for t in range(TPB):
                        ins = nc.tensor.transpose(ps[3][:, 256 * k + 128 * t:256 * k + 128 * t + 128],
                                                  sc[:, t, 128 * k:128 * k + 128], ident[:])
                ins.then_inc(W.a_ptr, 1)
                pe.wait_ge(W.a_ptc, b + 1)
                for t in range(TPB):
                    for k in range(TPB):
                        ins = mm(ps[4][:, 128 * t:128 * t + 128], pt_a[:, k, 128 * t:128 * t + 128], xl[:, k, :],
                                 start=(k == 0), stop=(k == TPB - 1))
                ins.then_inc(W.a_av, 1)
            with pe.Fori(0, B) as b:
                pe.wait_ge(W.a_xl, b + (B + 1))
                for t in range(TPB):
                    ins = nc.tensor.transpose(ps[0][:, 128 * t:128 * t + 128], xl[:, t, :], ident[:])
                ins.then_inc(W.y_tr, 1)
                pe.wait_ge(W.y_out, b + 1)

            pe.wait_ge(W.consts, 1)
            pe.wait_ge(W.mask_ready, 2)
            pe.wait_ge(W.lo_ready, G)
            pe.wait_ge(W.zeroed, 1)

            def body(n0, i0, s1, s3):
                for c in range(RING):
                    n, g, h = n0 + c, c % G, c // G
                    i = i0 + h
                    proj = live(n) and s1 is not None
                    fb = i - LAG_F
                    units = fb * FU + 2 * g

                    def attend(e):
                        m = n - LAG_PV
                        if not live(m):
                            return
                        if e == 0:
                            wait(pe, W.t_out, m + 1)
                            wait(pe, W.v_out, m * 2 + 2)
                        wait(pe, W.o_out, m * 4 - 2 + 2 * e)
                        rows = slice(64 * e, 64 * e + 64)
                        for hp in range(2):
                            for t in range(4):
                                col = (hp * 4 + t) * 64
                                ins = mm(p_o[e][:, col:col + 64], vring[rows, c, t, 128 * hp:128 * hp + 128],
                                         pt[rows, t, 64 * hp:64 * hp + 64], start=True, stop=True)
                        ins.then_inc(W.pv_done, 1)

                    def project(s):
                        wait(pe, W.rot_done, n * 4 - 2 + 2 * s)
                        xh, xl_ = xs_hi[:, h, WIN:], xs_lo[:, h, WIN:]
                        for half in range(2):
                            ins = split3(p_qk[s][:, S * half:S * half + S], qk_hi[:, g, s, half, :],
                                         qk_lo[:, g, s, half, :], xh, xl_)
                        ins.then_inc(W.qk_done, 1)

                    def values(k):
                        wait(pe, W.v_out, n * 2 + k)
                        for t in (2 * k, 2 * k + 1):
                            toks = slice(128 * (t // 2) + WIN * (t % 2), 128 * (t // 2) + WIN * (t % 2) + 128)
                            ins = split3(p_v[:, 256 * (t - 2 * k):256 * (t - 2 * k) + 256], xs_hi[:, h, toks],
                                         xs_lo[:, h, toks], v_hi[:, g, :], v_lo[:, g, :])
                        ins.then_inc(W.v_done, 1)

                    def feed(late):
                        u = 2 * g + late
                        wait(pe, W.f_free, fb * FU + u + 1)
                        if u == 0:
                            wait(pe, W.o_out, fb * (4 * G) + 4 * G)
                            if g == 0:
                                wait(pe, W.wo_load, wo_count)
                            for k in range(2 * G):
                                ins = mm(rb[:, 0:S], wo[:, k, :], ot[:, G * h + k // 2, k % 2, :],
                                         start=(k == 0), stop=(k == 2 * G - 1))
                        elif u == 1:
                            wait(pe, W.fx_ready, fb * 2 + 2)
                            ins = mm(rb[:, 0:S], mean[:], f_xs[:], start=True, stop=True)
                        elif u == 2:
                            wait(pe, W.fsq_ready, fb + 1)
                            for t in range(TPB):
                                ins = mm(rb[:, t:t + 1], f_sq[:, 128 * t:128 * t + 128], mean[:, 0:1],
                                         start=True, stop=True)
                        elif u == 3:
                            wait(pe, W.lnewton, fb * NEWTON + NEWTON)
                            for t in range(TPB):
                                for k in range(3):
                                    ins = mm(rb[:, 128 * t:128 * t + 128],
                                             rl_parts[:, k, t:t + 1].to_broadcast([128, 128]),
                                             ident_b[:], start=(k == 0), stop=(k == 2))
                        elif u < 7:
                            k = u - 4
                            wait(pe, W.fn_lo, fb + 1)
                            if k == 0:
                                wait(pe, W.w1lo_ready, w1_count)
                            for v in range(2):
                                ins = split3(rb[0:FCH[k], S * v:S * v + S], w1_hi[:, k, v, 0:FCH[k]],
                                             w1_lo[:, k, v, 0:FCH[k]], f_hi[:], f_lo[:])
                        else:
                            for k, w in enumerate(FCH):
                                ins = mm(rb[:, 0:S], w2[0:w, k, :], hid[0:w, k, :], start=(k == 0), stop=(k == 2))
                        ins.then_inc(W.f_done, 1)

                    attend(0)
                    if live(n - 1):
                        wait(pe, W.sq_summed, n)
                        if isinstance(units, int) and units <= 0:
                            wait(pe, W.r_used, (n - 1 - LAG_R) * 2 + 2)
                            wait(pe, W.n_copied, n - 1)
                        else:
                            wait(pe, W.f_free, units + 1)
                            if c == 0:
                                wait(pe, W.r_used, (n - 1 - LAG_R) * 2 + 2)
                        for s in range(2):
                            at = 32 - HPG - (s * HEADS + HPG * ((g - 1) % G))
                            ins = mm(rb[0:96, 0:S], sel[:, at:at + 96], squares[:, s, 0, :],
                                     start=(s == 0), stop=(s == 1))
                        ins.then_inc(W.n_done, 1)
                    if proj:
                        if g == 0:
                            wait(pe, W.xs_ready, i * 2 + 2)
                        project(0)
                        values(0)
                    attend(1)
                    m = n - LAG_T
                    if live(m):
                        wait(pe, W.scaled, m + 1)
                        wait(pe, W.t_out, m)
                        pm = probs[:, (c - LAG_T) % 2, :, :].rearrange("p w k -> p (w k)")
                        for t in range(4):
                            ins = nc.tensor.transpose(p_t[:, 128 * t:128 * t + 128], pm[:, 128 * t:128 * t + 128],
                                                      ident[:])
                        ins.then_inc(W.t_done, 1)
                    if s3 is not None:
                        if live(n - 1):
                            wait(pe, W.n_copied, n)
                        feed(0)
                    m = n - LAG_S
                    if live(m):
                        wait(pe, W.centred, m)
                        wait(pe, W.r_used, m * 2 + 2)
                        wait(pe, W.spread, m * 64 + 64)
                        slot_k, slot_q = (c - LAG_S) % RING, (c - LAG_S + LAG_R) % 2
                        ins = mm(p_s[:], ident_b[:], wmask[:], start=True, stop=False, skip_group_check=True)
                        for w in range(NW):
                            lo = max(0, w - 1) * WIN
                            hi = (w + 1) * WIN
                            end = 2 * WIN * (ORDER.index(w) + 1)
                            dst = p_s[:, end - (hi - lo):end]
                            for half in range(2):
                                ins = mm(dst, qbd[:, slot_q, half, w, :, :].rearrange("p j t -> p (j t)"),
                                         rotated[:, slot_k, 1, half, lo:hi], start=False,
                                         stop=(w == NW - 1 and half == 1), skip_group_check=True)
                        ins.then_inc(W.s_done, 1)
                    m = n - LAG_R
                    if live(m):
                        if s3 is not None:
                            wait(pe, W.f_free, units + 1 + 1)
                        else:
                            wait(pe, W.n_copied, n)
                        if g == 1:
                            wait(pe, W.newton, i * ROOT)
                        for s in range(2):
                            ins = mm(rb2[:, s, :], r_sel[:, s * G + (g - LAG_R) % G, :], r_rows[:],
                                     start=True, stop=True)
                        ins.then_inc(W.r_done, 1)
                    if proj:
                        project(1)
                    if proj:
                        values(1)
                    if s3 is not None:
                        if live(n - LAG_R):
                            wait(pe, W.r_used, (n - LAG_R) * 2 + 2)
                        feed(1)

            wo_count, w1_count = 16, 1

            def reload_projection(layer):
                wait_apart(pe, W.lo_ready, (layer + 2) * G, W.zeroed)

            def reload_rest(layer):
                wait_apart(pe, W.wo_load, (layer + 2) * 16, W.zeroed)
                wait_apart(pe, W.rest_load, (layer + 2) * 48, W.zeroed)
                wait_apart(pe, W.w1lo_ready, layer + 2, W.zeroed)

            pe.wait_ge(W.wo_load, 16)
            pe.wait_ge(W.rest_load, 48)
            schedule(pe, body, reload_projection, reload_rest)

            with pe.Fori(0, B) as b:
                pe.wait_ge(W.fin_copy, b + 1)
                wait(pe, W.fin_add, b + 1)
                for t in range(TPB):
                    ins = nc.tensor.transpose(ps[0][:, 128 * t:128 * t + 128], x_fin[:, 128 * t:128 * t + 128],
                                              ident[:])
                ins.then_inc(W.fin_tr, 1)

        @block.vector
        def _(dve):
            v = nc.vector

            def inverse_root(s, y, t, parts, done, base):
                step = [0]

                def link(ins):
                    step[0] += 1
                    ins.then_inc(done, 1)
                    dve.wait_ge(done, base + step[0])
                link(v.tensor_scalar(y.bitcast(I32), s.bitcast(I32), -0.5, MAGIC, ALU.mult, ALU.add))
                for _ in range(3):
                    link(v.tensor_tensor(t, y, y, ALU.mult))
                    link(v.scalar_tensor_tensor(t, t, -0.5, s, ALU.mult, ALU.mult))
                    link(v.scalar_tensor_tensor(y, t, 1.5, y, ALU.add, ALU.mult))
                if parts is not None:
                    link(v.tensor_copy(parts[0], y))
                    link(v.tensor_tensor(t, y, parts[0], ALU.subtract))
                    link(v.tensor_copy(parts[1], t))
                    link(v.tensor_tensor(parts[2], t, parts[1], ALU.subtract))

            dve.wait_ge(W.cload, 16 * CLOADS)
            v.tensor_copy(r_sel[:], r_sel_f).then_inc(W.mask_ready, 1)
            v.tensor_copy(ident_b[:], ident[:]).then_inc(W.consts, 1)
            v.tensor_copy(wmask[:], wmask_f).then_inc(W.mask_ready, 1)

            def layer_norm(k):
                base = 3 * k
                v.tensor_reduce(st[:, 0, :], x_tok, AX.X, ALU.add).then_inc(W.stats, 1)
                dve.wait_ge(W.stats, base + 1)
                v.tensor_scalar(st[:, 0, :], st[:, 0, :], 1.0 / D, None, ALU.mult).then_inc(W.stats, 1)
                dve.wait_ge(W.stats, base + 2)
                v.tensor_tensor(xc_tok, x_tok, st[:, 0, :].unsqueeze(2).to_broadcast([128, NT, D]),
                                ALU.subtract).then_inc(W.a_dve, 1)
                dve.wait_ge(W.a_step, k + 1)
                v.tensor_reduce(st[:, 1, :], sq_tok, AX.X, ALU.add).then_inc(W.stats, 1)
                dve.wait_ge(W.stats, base + 3)
                v.tensor_scalar(st[:, 1, :], st[:, 1, :], 1.0 / D, LN_EPS, ALU.mult, ALU.add).then_inc(W.one_step, 1)
                dve.wait_ge(W.one_step, k + 1)
                inverse_root(st[:, 1, :], st[:, 2, :], st[:, 3, :], None, W.m_step, 10 * k)

            def normed(b):
                return v.tensor_tensor(xl, xc_tok.rearrange("p (b t) d -> p b t d", t=TPB)[:, b, :, :],
                                       st[:, 2, :].rearrange("p (b t) -> p b t", t=TPB)[:, b, :]
                                       .unsqueeze(2).to_broadcast([128, TPB, D]), ALU.mult)

            for c in range(4):
                dve.wait_ge(W.x_load, 64)
            layer_norm(0)
            x_b = x_tok.rearrange("p (b t) d -> p b t d", t=TPB)
            with dve.Fori(0, B) as b:
                dve.wait_ge(W.a_av, b + 1)
                normed(b).then_inc(W.a_xl, 1)
                dve.wait_ge(W.a_sc, b + 1)
                ps2 = ps[2][:].rearrange("p (t k) -> p t k", t=TPB)
                v.tensor_tensor(sc, ps2, cmask[:, 0, :, :], ALU.mult).then_inc(W.a_masked, 1)
                dve.wait_ge(W.a_masked, 2 * b + 1)
                v.tensor_tensor(sc, sc, cmask[:, 1, :, :], ALU.add).then_inc(W.a_masked, 1)
                dve.wait_ge(W.a_masked, 2 * b + 2)
                v.tensor_reduce(amx, sc, AX.X, ALU.max, negate=True).then_inc(W.a_max, 1)
                dve.wait_ge(W.a_exp, 2 * b + 2)
                v.reciprocal(arec, asum).then_inc(W.a_rec, 1)
                dve.wait_ge(W.a_rec, b + 1)
                dve.wait_ge(W.a_av, b + 1 + 1)
                for t in range(TPB):
                    xt = x_b[:, b, t, :]
                    v.scalar_tensor_tensor(xt, ps[4][:, 128 * t:128 * t + 128], arec[:, t:t + 1], xt,
                                           ALU.mult, ALU.add).then_inc(W.a_x1, 1)
            dve.wait_ge(W.a_x1, 2 * B)
            layer_norm(1)
            with dve.Fori(0, B) as b:
                wait(dve, W.y_tr, b + 1)
                normed(b).then_inc(W.a_xl, 1)

            def split_projection(count):
                for g in range(G):
                    dve.wait_ge(W.hi_ready, count * (3 * G) + 3 * g + 3)
                    for s in range(2):
                        src = raw[:, INNER * s + 256 * g:INNER * s + 256 * g + 256].rearrange(
                            "p (h x f) -> p x h f", h=HPG, x=2)
                        hi = qk_hi[:, g, s, :, :].bitcast(F32).rearrange("p x (h f) -> p x h f", h=HPG)
                        lo = qk_lo[:, g, s, :, :].rearrange("p x (h f) -> p x h f", h=HPG)
                        v.tensor_tensor(lo, src, hi, ALU.subtract)
                    v.tensor_tensor(v_lo[:, g, :], raw[:, 2 * INNER + 256 * g:2 * INNER + 256 * g + 256],
                                    v_hi[:, g, :].bitcast(F32), ALU.subtract).then_inc(W.lo_ready, 1)

            def tables(layer, count):
                v.tensor_copy(qks[:], qks_all[:, layer, :]).then_inc(W.tab_ready, 1)
                dve.wait_ge(W.tab_ready, count * 9 + 1)
                for s in range(2):
                    for half in range(2):
                        v.tensor_scalar(tab[:, s, 0, half, :], rot[:, 2 * s, :], qks[:, 2 * s + half:2 * s + half + 1],
                                        None, ALU.mult).then_inc(W.tab_ready, 1)
                        v.tensor_scalar(tab[:, s, 1, half, :], rot[:, 2 * s + 1, :],
                                        qks[:, 2 * s + 1 - half:2 * s + 2 - half], -1.0 if half == 0 else 1.0,
                                        ALU.mult, ALU.mult).then_inc(W.tab_ready, 1)
                wait_apart(dve, W.tab_ready, count * 9 + 9, W.zeroed)

            def split_w1(count):
                dve.wait_ge(W.w1hi_ready, count * 6 + 6)
                for k, w in enumerate(FCH):
                    for g in range(2):
                        off = (FF if g == 0 else 0) + 128 * k
                        ins = v.tensor_tensor(w1_lo[:, k, g, 0:w], w1_raw[:, off:off + w],
                                              w1_hi[:, k, g, 0:w].bitcast(F32), ALU.subtract)
                ins.then_inc(W.w1lo_ready, 1)

            def vectors(layer, count):
                v.tensor_copy(vecs[:], vecs_all[:, layer, :]).then_inc(W.vec_ready, 1)
                wait_apart(dve, W.vec_ready, count + 1, W.zeroed)

            def shift_rest(batch, h, count):
                wait(dve, W.fc_ready, count * 2 + 2)
                for lo in (0, 64):
                    rows = slice(lo, lo + 64)
                    off = 1 - lo // 64
                    v.tensor_tensor(xs_lo[rows, h, WIN:], X[rows, batch, off:off + S],
                                    xs_hi[rows, h, WIN:].bitcast(F32), ALU.subtract).then_inc(W.xs_ready, 1)

            split_projection(0)
            tables(0, 0)
            split_w1(0)
            vectors(0, 0)
            dve.wait_ge(W.x1_saved, 16)
            dve.wait_ge(W.zeroed, 1)
            dve.wait_ge(W.y_out, B)
            shift_rest(0, 0, 0)

            def body(n0, i0, s1, s3):
                for c in range(RING):
                    n, g, h = n0 + c, c % G, c // G
                    i = i0 + h
                    proj = live(n) and s1 is not None
                    fb = i - LAG_F

                    def turn(s):
                        wait(dve, W.sq_done, n * 2 + 1 + s)
                        wait(dve, W.added, n * 2 + s)
                        if s == 1:
                            wait(dve, W.s_done, n - RING + 1)
                        src = p_qk[s][:].rearrange("p (x t) -> p x t", x=2)
                        v.tensor_tensor(rotated[:, c, s, :, :], src, tab[:, s, 0, :, :], ALU.mult
                                        ).then_inc(W.rot_done, 1)
                        v.tensor_tensor(turned[:], src[:, ::-1, :], tab[:, s, 1, :, :], ALU.mult
                                        ).then_inc(W.rot_done, 1)

                    def feed(late):
                        u = 2 * g + late
                        pair = s3 * 2 + h
                        wait(dve, W.f_done, fb * FU + u + 1)
                        xb = X[:, pair, 1:S + 1]
                        if u == 0:
                            v.tensor_tensor(xb, rb[:, 0:S], xb, ALU.add).then_inc(W.f_free, 1)
                        elif u == 1:
                            v.tensor_tensor(f_xc[:], f_xs[:], rb[:, 0:S], ALU.subtract).then_inc(W.f_free, 1)
                        elif u == 2:
                            v.tensor_scalar(lv[:, 0, :], rb[:, 0:TPB], LN_EPS, None, ALU.add).then_inc(W.f_free, 1)
                            dve.wait_ge(W.f_free, fb * FU + 3 + 1)
                            inverse_root(lv[:, 0, :], lv[:, 1, :], lv[:, 2, :],
                                         [rl_parts[:, k, :] for k in range(3)], W.lnewton, fb * NEWTON)
                        elif u == 3:
                            v.tensor_tensor(f_xc[:], f_xc[:], rb[:, 0:S], ALU.mult).then_inc(W.f_free, 1)
                            dve.wait_ge(W.f_free, fb * FU + 4 + 1)
                            v.tensor_scalar(f_xc[:], f_xc[:], vecs[:, 0:1], vecs[:, 1:2], ALU.mult, ALU.add
                                            ).then_inc(W.fn_ready, 1)
                        elif u < 7:
                            k = u - 4
                            w = FCH[k]
                            dve.wait_ge(W.gelu_done, fb * 3 + k + 1)
                            v.scalar_tensor_tensor(hid[0:w, k, :], rb[0:w, S:2 * S], vecs[0:w, 6 + k:7 + k],
                                                   f_sq[0:w, :], ALU.add, ALU.mult).then_inc(W.f_free, 1)
                        else:
                            v.scalar_tensor_tensor(xb, rb[:, 0:S], vecs[:, 2:3], xb, ALU.add, ALU.add
                                                   ).then_inc(W.f_free, 1)

                    def root(first, last):
                        if g != 0 or not live(n - 1):
                            return
                        for k in range(first, last):
                            if k == 0:
                                wait(dve, W.n_copied, n)
                                ins = v.tensor_scalar(norm[:], norm[:], 1e-24, None, ALU.max)
                            elif k == 1:
                                ins = v.tensor_scalar(nt_y[:].bitcast(I32), norm[:].bitcast(I32), -0.5, MAGIC,
                                                      ALU.mult, ALU.add)
                            elif k < 11 and k % 3 == 2:
                                ins = v.tensor_tensor(nt_t[:], nt_y[:], nt_y[:], ALU.mult)
                            elif k < 11 and k % 3 == 0:
                                ins = v.scalar_tensor_tensor(nt_t[:], nt_t[:], -0.5, norm[:], ALU.mult, ALU.mult)
                            elif k < 11:
                                ins = v.scalar_tensor_tensor(nt_y[:], nt_t[:], 1.5, nt_y[:], ALU.add, ALU.mult)
                            elif k == 11:
                                ins = v.tensor_copy(r_rows[:], nt_y[:])
                            elif k == 12:
                                ins = v.tensor_tensor(nt_t[:], nt_y[:], r_rows[:], ALU.subtract)
                            elif k == 13:
                                v.tensor_copy(r_rows[32:64, :], nt_t[32:64, :])
                                ins = v.tensor_copy(r_rows[64:96, :], nt_t[64:96, :])
                            else:
                                ins = v.tensor_tensor(r_rows[64:96, :], nt_t[64:96, :], r_rows[64:96, :],
                                                      ALU.subtract)
                            ins.then_inc(W.newton, 1)
                            if k < ROOT - 1:
                                dve.wait_ge(W.newton, (i - 1) * ROOT + k + 1)

                    if live(n - 1):
                        wait(dve, W.n_done, n)
                        if g == 1:
                            wait(dve, W.newton, i * ROOT)
                            v.tensor_copy(norm[:], rb[0:96, 0:S]).then_inc(W.n_copied, 1)
                        else:
                            v.tensor_tensor(norm[:], rb[0:96, 0:S], norm[:], ALU.add).then_inc(W.n_copied, 1)
                    root(0, 5)
                    if proj:
                        turn(0)
                    root(5, 8)
                    if s3 is not None:
                        feed(0)
                    root(8, 11)
                    m = n - LAG_R
                    if live(m):
                        slot = (c - LAG_R) % RING
                        wait(dve, W.r_done, m + 1)
                        wait(dve, W.added, m * 2 + 2)
                        wait(dve, W.spread, m * 64)
                        for s in range(2):
                            src = rotated[:, slot, s, :, :]
                            v.tensor_tensor(qr[:] if s == 0 else src, src,
                                            rb2[:, s, :].unsqueeze(1).to_broadcast([128, 2, S]), ALU.mult
                                            ).then_inc(W.r_used, 1)
                    m = n - LAG_S
                    if live(m):
                        wait(dve, W.s_done, m + 1)
                        sc3 = p_s[:].rearrange("p (w k) -> p w k", w=NW)
                        v.tensor_reduce(top[:], sc3, AX.X, ALU.max).then_inc(W.top_done, 1)
                        wait(dve, W.top_done, m + 1)
                        wait(dve, W.t_done, m - 1)
                        v.tensor_tensor(probs[:, (c - LAG_S) % 2, :, :], sc3,
                                        top[:].unsqueeze(2).to_broadcast([128, NW, 2 * WIN]), ALU.subtract
                                        ).then_inc(W.centred, 1)
                    if s3 is not None:
                        feed(1)
                    if proj:
                        turn(1)
                    if live(m):
                        slot = (c - LAG_S) % 2
                        wait(dve, W.exp_done, m + 1)
                        v.tensor_reduce(total[:, 0, :], probs[:, slot, :, :], AX.X, ALU.add).then_inc(W.summed, 1)
                        wait(dve, W.summed, m + 1)
                        wait(dve, W.scaled, m)
                        v.reciprocal(total[:, 1, :], total[:, 0, :]).then_inc(W.total_done, 1)
                    root(11, ROOT)
                    if proj and g == 2:
                        shift_rest(s1 * 2 + 1 if h == 0 else (s1 * 2 + 2) % B, 1 - h, i + 1)

            def reload_projection(layer):
                split_projection(layer + 1)
                tables(layer + 1, layer + 1)

            def reload_rest(layer):
                split_w1(layer + 1)
                vectors(layer + 1, layer + 1)

            schedule(dve, body, reload_projection, reload_rest)
            dve.wait_ge(W.x1_loaded, 16)
            xb1 = x1_back.rearrange("p (b t) d -> p b t d", t=TPB)
            with dve.Fori(0, B) as b:
                dve.wait_ge(W.fin_tr, b + 1 + 1)
                v.tensor_tensor(xb1[:, b, :, :], xb1[:, b, :, :],
                                ps[0][:, 0:S].rearrange("p (t d) -> p t d", t=TPB), ALU.add).then_inc(W.fin_add, 1)

        @block.scalar
        def _(act):
            A = nc.scalar.activation

            def copy(dst, src):
                return A(dst, src, ACT.Copy)

            def layer_norm(k):
                act.wait_ge(W.a_dve, k + 1)
                A(sq_tok, xc_tok, ACT.Square).then_inc(W.a_step, 1)

            layer_norm(0)
            act.wait_ge(W.cload, 16 * CLOADS)
            with act.Fori(0, B) as b:
                act.wait_ge(W.a_tr, b + 1)
                copy(xl_t, ps[0][:, 0:S]).then_inc(W.a_trc, 1)
                act.wait_ge(W.a_qk, b + 1)
                for s in range(2):
                    A(qk_a[:, s, :], ps[1][0:E, 256 * s:256 * s + 256], ACT.Identity, bias=bqk[:, s:s + 1]
                      ).then_inc(W.a_qkc, 1)
                act.wait_ge(W.a_max, b + 1)
                for t in range(TPB):
                    A(sc[:, t, :], sc[:, t, :], ACT.Exp, bias=amx[:, t:t + 1], accum_out=asum[:, t:t + 1]
                      ).then_inc(W.a_exp, 1)
                act.wait_ge(W.a_ptr, b + 1)
                copy(pt_a, ps[3][:].rearrange("p (k q) -> p k q", k=TPB)).then_inc(W.a_ptc, 1)
            layer_norm(1)
            act.wait_ge(W.zeroed, 1)
            with act.Fori(0, B) as b:
                act.wait_ge(W.y_tr, b + 1 + 1)
                copy(X[:, b, 1:S + 1], ps[0][:, 0:S]).then_inc(W.y_out, 1)

            def split_projection(count, done):
                act.wait_ge(W.wload, (count + 1) * 16)
                if done is not None:
                    act.wait_ge(W.v_done, done)
                for g in range(G):
                    for s in range(2):
                        src = raw[:, INNER * s + 256 * g:INNER * s + 256 * g + 256].rearrange(
                            "p (h x f) -> p x h f", h=HPG, x=2)
                        copy(qk_hi[:, g, s, :, :].rearrange("p x (h f) -> p x h f", h=HPG), src
                             ).then_inc(W.hi_ready, 1)
                    copy(v_hi[:, g, :], raw[:, 2 * INNER + 256 * g:2 * INNER + 256 * g + 256]).then_inc(W.hi_ready, 1)

            def shift_split(batch, h):
                for lo in (0, 64):
                    rows = slice(lo, lo + 64)
                    off = 1 - lo // 64
                    copy(xs_hi[rows, h, WIN:], X[rows, batch, off:off + S]).then_inc(W.fc_ready, 1)

            def split_w1(count):
                act.wait_ge(W.rest_load, (count + 1) * 48)
                for k, w in enumerate(FCH):
                    for g in range(2):
                        off = (FF if g == 0 else 0) + 128 * k
                        copy(w1_hi[:, k, g, 0:w], w1_raw[:, off:off + w]).then_inc(W.w1hi_ready, 1)

            split_projection(0, None)
            split_w1(0)
            act.wait_ge(W.vec_ready, 1)
            act.wait_ge(W.y_out, B)
            shift_split(0, 0)

            def body(n0, i0, s1, s3):
                for c in range(RING):
                    n, g, h = n0 + c, c % G, c // G
                    i = i0 + h
                    proj = live(n) and s1 is not None
                    fb = i - LAG_F

                    def square(s):
                        wait(act, W.qk_done, n * 2 + 1 + s)
                        wait(act, W.n_done, n)
                        A(squares[:, s, :, :], p_qk[s][:].rearrange("p (x t) -> p x t", x=2), ACT.Square
                          ).then_inc(W.sq_done, 1)

                    def values(k):
                        wait(act, W.v_done, n * 2 + 1 + k)
                        wait(act, W.pv_done, (n - RING) * 2 + 2)
                        copy(vring[:, c, 2 * k:2 * k + 2, :], p_v[:].rearrange("p (t d) -> p t d", t=2)
                             ).then_inc(W.v_out, 1)

                    def feed(late):
                        u = 2 * g + late
                        if u == 1:
                            wait(act, W.f_free, fb * FU + 2 + 1)
                            A(f_sq[:], f_xc[:], ACT.Square).then_inc(W.fsq_ready, 1)
                        elif 4 <= u < 7:
                            k = u - 4
                            w = FCH[k]
                            wait(act, W.f_done, fb * FU + u + 1)
                            A(f_sq[0:w, :], rb[0:w, 0:S], ACT.Gelu, bias=vecs[0:w, 3 + k:4 + k]
                              ).then_inc(W.gelu_done, 1)

                    if proj:
                        square(0)
                        values(0)
                    m = n - LAG_PV
                    if live(m):
                        wait(act, W.f_done, (i - 4) * FU + 1)
                        for e in range(2):
                            wait(act, W.pv_done, m * 2 + 1 + e)
                            for k in range(2):
                                rows = slice(64 * k, 64 * k + 64)
                                src = p_o[e][rows, :].rearrange("p (a t x) -> p a t x", t=2, x=2 * WIN)[
                                    :, :, :, WIN * k:WIN * k + WIN]
                                dst = ot[rows, c, :, :].rearrange("p a t -> p (a t)").rearrange(
                                    "p (a e t x) -> p a e t x", e=2, t=2, x=WIN)[:, :, e, :, :]
                                copy(dst, src).then_inc(W.o_out, 1)
                    m = n - LAG_T
                    if live(m):
                        wait(act, W.t_done, m + 1)
                        wait(act, W.pv_done, m * 2)
                        copy(pt[:], p_t[:].rearrange("p (t x) -> p t x", t=4)
                             ).then_inc(W.t_out, 1)
                    if s3 is not None:
                        feed(0)
                    if s3 is not None and g == 0:
                        wait(act, W.f_free, fb * FU + 1 + 1)
                        for lo in (0, 64):
                            rows = slice(lo, lo + 64)
                            off = 1 - lo // 64
                            copy(f_xs[rows, :], X[rows, s3 * 2 + h, off:off + S]).then_inc(W.fx_ready, 1)
                    if proj:
                        square(1)
                    m = n - LAG_S
                    if live(m):
                        slot = (c - LAG_S) % 2
                        wait(act, W.centred, m + 1)
                        A(probs[:, slot, :, :], probs[:, slot, :, :], ACT.Exp).then_inc(W.exp_done, 1)
                    if proj:
                        values(1)
                        if g == 1:
                            wait(act, W.f_free, (i - 4) * FU + 1)
                            wait(act, W.v_done, i * (2 * G))
                            shift_split(s1 * 2 + 1 if h == 0 else (s1 * 2 + 2) % B, 1 - h)
                    if s3 is not None:
                        feed(1)

            def reload_projection(layer):
                split_projection(layer + 1, (layer + 1) * (2 * B * G))

            def reload_rest(layer):
                split_w1(layer + 1)
                act.wait_ge(W.vec_ready, layer + 2)

            schedule(act, body, reload_projection, reload_rest)
            act.wait_ge(W.f_free, DEPTH * B * FU + 1)
            with act.Fori(0, B) as b:
                wait(act, W.fin_tr, b + 1)
                copy(x_fin, X[:, b, 1:S + 1]).then_inc(W.fin_copy, 1)

        @block.gpsimd
        def _(pool):
            gp = nc.gpsimd
            for first in (W.f_free, W.a_av, W.y_tr, W.fin_add, W.fin_tr):
                pool.sem_inc(first, 1)
            gp.memset(X[:, :, 0:1], 0.0).then_inc(W.pool_zero, 1)
            gp.memset(xs_hi[:, :, 0:WIN].bitcast(F32), 0.0).then_inc(W.pool_zero, 1)
            gp.memset(xs_lo[:, :, 0:WIN].bitcast(F32), 0.0).then_inc(W.pool_zero, 1)
            gp.memset(qbd[:], 0.0).then_inc(W.pool_zero, 1)
            pool.wait_ge(W.pool_zero, 4)
            gp.memset(top[:], 0.0).then_inc(W.zeroed, 1)

            def body(n0, i0, s1, s3):
                for c in range(RING):
                    n, g, h = n0 + c, c % G, c // G
                    i = i0 + h
                    proj = live(n) and s1 is not None
                    fb = i - LAG_F

                    def add(s):
                        wait(pool, W.rot_done, n * 4 + 2 + 2 * s)
                        x = rotated[:, c, s, :, :]
                        gp.tensor_tensor(x, x, turned[:], ALU.add).then_inc(W.added, 1)

                    if proj:
                        add(0)
                        wait(pool, W.sq_done, n * 2 + 2)
                        gp.tensor_tensor(squares[:, :, 0, :], squares[:, :, 0, :], squares[:, :, 1, :], ALU.add
                                         ).then_inc(W.sq_summed, 1)
                        add(1)
                    m = n - LAG_S
                    if live(m):
                        wait(pool, W.total_done, m + 1)
                        x = probs[:, (c - LAG_S) % 2, :, :]
                        gp.tensor_tensor(x, x, total[:, 1, :].unsqueeze(2).to_broadcast([128, NW, 2 * WIN]),
                                         ALU.mult).then_inc(W.scaled, 1)
                    if s3 is not None and g == 1:
                        wait_apart(pool, W.fn_ready, fb + 1, W.zeroed)
                        gp.tensor_copy(f_hi[:], f_xc[:]).then_inc(W.fn_hi, 1)
                        wait(pool, W.fn_hi, fb + 1)
                        gp.tensor_tensor(f_lo[:], f_xc[:], f_hi[:].bitcast(F32), ALU.subtract).then_inc(W.fn_lo, 1)

            schedule(pool, body, lambda layer: None, lambda layer: None)


CLOADS = 11

_INS = ['L0_attn_x', 'L0_ffn_Wqkv', 'L0_ffn_Wo', 'L0_ffn_W1', 'L0_ffn_W2']


def lay_out(x):
    got = {"wqk_t": np.stack([np.asarray(x["L0_attn_w_q"]).T, np.asarray(x["L0_attn_w_k"]).T], 1),
           "bqk": np.stack([np.asarray(x["L0_attn_b_q"]), np.asarray(x["L0_attn_b_k"])], 1)}
    qks = [np.asarray(x[w]).reshape(DEPTH, 2, HALF).transpose(2, 0, 1) for w in ("L0_ffn_q_scale", "L0_ffn_k_scale")]
    got["qks"] = np.tile(np.concatenate(qks, 2), (HPG, 1, 1))
    vecs = np.zeros((128, DEPTH, 9), np.float32)
    for k, w in enumerate(("L0_ffn_ln_g", "L0_ffn_ln_b", "L0_ffn_b2")):
        vecs[:, :, k] = np.asarray(x[w]).T
    b1 = np.asarray(x["L0_ffn_b1"])
    for k, off in ((3, FF), (6, 0)):
        for c, m in enumerate(FCH):
            vecs[0:m, :, k + c] = b1[:, off + 128 * c:off + 128 * c + m].T
    got["vecs"] = vecs
    return {n: np.ascontiguousarray(v) for n, v in got.items()}


def kernel(**inputs):
    import numpy as _np
    import concourse.bacc as _bacc
    from concourse import mybir as _mybir
    from concourse.bass_utils import run_bass_kernel_spmd as _run

    nc = _bacc.Bacc("TRN2", target_bir_lowering=False, num_devices=1)
    values = {name: _np.ascontiguousarray(inputs[name]) for name in _INS}
    values.update(lay_out(inputs))
    values.update(constants())
    arrays, handles = {}, {}
    for name, value in values.items():
        arrays[f"in_{name}"] = value
        handles[name] = nc.dram_tensor(f"in_{name}", value.shape, _mybir.dt.from_np(value.dtype),
                                       kind="ExternalInput").ap()
    out = nc.dram_tensor("out_0", (B, S, D), F32, kind="ExternalOutput").ap()
    build(nc, handles, out)
    r = _run(nc, [arrays], core_ids=[0])
    return r.results[0]["out_0"]
```

```python
from contextlib import ExitStack

import numpy as np
import concourse.bass as bass
from concourse import mybir

F32 = mybir.dt.float32
F32R = mybir.dt.float32r
BF16 = mybir.dt.bfloat16
I32 = mybir.dt.int32
ALU = mybir.AluOpType
ACT = mybir.ActivationFunctionType
AX = mybir.AxisListType

B, S, D = 16, 256, 128
E = 16
DEPTH, HEADS, DH, WIN = 6, 16, 64, 32
INNER = HEADS * DH
NW = S // WIN
HALF = DH // 2
HPG = 4
G = HEADS // HPG
FF = int(D * 4 * 2 / 3)
FCH = [min(128, FF - c * 128) for c in range((FF + 127) // 128)]
NT = B * S // 128
TPB = S // 128
RING = 2 * G
CLOCKS = DEPTH * B * G
PAIRS = B // 2
LAG_R, LAG_S, LAG_T, LAG_PV = 5, 6, 7, 8
LAG_F = 4
FU = 8
NEWTON = 14
ROOT = 15
MAGIC = float(0x5F3759DF)
LN_EPS = 1e-5
MASKED = -1e30
SEL = 32 - HPG + 96
ORDER = [0, 2, 1, 3, 4, 6, 5, 7]
NEG = -10000.0


def constants():
    c = {}
    c["ident"] = np.eye(128, dtype=np.float32)
    p = np.arange(128)
    at = np.arange(SEL)[None] - (32 - HPG)
    c["sel"] = ((at >= 0) & (at % 32 == p[:, None] // HALF)).astype(np.float32)
    c["mean"] = np.full((128, 128), 1.0 / D, np.float32)
    row = np.arange(96)[:, None, None] % 32
    c["spread"] = (row == (HPG * np.arange(2 * G)[None, :, None] + p[None, None, :] // HALF)).astype(np.float32)
    a, b = (p % WIN)[:, None], np.arange(WIN)[None]
    prev = np.where(a > b, MASKED, 0.0)
    own = np.where(a < b, MASKED, 0.0)
    m = np.zeros((128, NW, 2, WIN))
    m[:, :, 0] = prev[:, None]
    m[:, 0, 0] = MASKED
    m[:, :, 1] = own[:, None]
    m = m[:, ORDER]
    c["wmask"] = m.reshape(128, NW * 2 * WIN).astype(np.float32)
    half = np.arange(0, DH, 2, dtype=np.float32)
    inv_freq = (1.0 / 10000.0 ** (half / DH)).astype(np.float32)
    t = np.arange(S, dtype=np.float32)
    freqs = (t[:, None] * inv_freq[None, :]).astype(np.float32)
    base = ((half + 0.4 * DH) / (1.4 * DH)).astype(np.float32)
    scale = (base[None, :] ** ((t - S // 2) / (WIN // 2))[:, None]).astype(np.float32)
    cos, sin = np.cos(freqs), np.sin(freqs)
    tabs = [cos * scale * 8.0, sin * scale * 8.0, cos * (1 / scale), sin * (1 / scale)]
    c["rot"] = np.stack([np.tile(x.T, (HPG, 1)) for x in tabs], 1).astype(np.float32)
    q = (p[:, None] + 128 * np.arange(TPB)[None])[:, :, None]
    seen = q >= np.arange(S)[None, None]
    c["cmask"] = np.stack([np.where(seen, 0.25, 0.0), np.where(seen, 0.0, NEG)], 1).astype(np.float32)
    return c


CONST_NAMES = ["ident", "sel", "mean", "wmask", "rot", "cmask"]


def live(m):
    return not isinstance(m, int) or 0 <= m < CLOCKS


def wait(eng, sem, value):
    if isinstance(value, int) and value <= 0:
        return
    eng.wait_ge(sem, value)


def wait_apart(eng, sem, value, settled):
    if isinstance(value, int) and value <= 0:
        return
    if not isinstance(value, int):
        value = eng.to_reg(value)
    eng.wait_ge(settled, 1)
    eng.wait_ge(sem, value)


def schedule(eng, body, reload_projection, reload_rest):
    body(0, 0, 0, None)
    body(RING, 2, 1, None)
    with eng.Fori(0, DEPTH - 1) as layer:
        n_layer, i_layer = layer * (PAIRS * RING), layer * B
        with eng.Fori(2, PAIRS) as p:
            body(n_layer + p * RING, i_layer + p * 2, p, p - 2)
        reload_projection(layer)
        with eng.Fori(0, 2) as p:
            body(n_layer + p * RING + PAIRS * RING, i_layer + p * 2 + B, p, p + (PAIRS - 2))
        reload_rest(layer)
    n_last = (DEPTH - 1) * PAIRS * RING
    with eng.Fori(2, PAIRS) as p:
        body(p * RING + n_last, p * 2 + (DEPTH - 1) * B, p, p - 2)
    body(CLOCKS, DEPTH * B, None, PAIRS - 2)
    body(CLOCKS + RING, DEPTH * B + 2, None, PAIRS - 1)


def build(nc, a, out):
    with ExitStack() as ctx:
        def sb(name, shape, dt=F32):
            return ctx.enter_context(nc.sbuf_tensor(name, shape, dt))

        def sem(name):
            return ctx.enter_context(nc.semaphore(name))

        ps = [ctx.enter_context(nc.psum_tensor(f"bank{i}", [128, 512], F32)) for i in range(8)]
        p_qk, p_v, p_t, p_s, p_o, p_rb = ps[0:2], ps[2], ps[3], ps[4], ps[5:7], ps[7]
        x1_dram = nc.dram_tensor("x1_scratch", [128, NT, D], F32, kind="Internal").ap()

        X = sb("X", [128, B, S + 1])
        raw = sb("raw", [128, 3 * INNER])
        qk_hi = sb("qk_hi", [128, G, 2, 2, 128], F32R)
        qk_lo = sb("qk_lo", [128, G, 2, 2, 128], F32R)
        v_hi = sb("v_hi", [128, G, 256], F32R)
        v_lo = sb("v_lo", [128, G, 256], F32R)
        wo = sb("wo", [128, 2 * G, D])
        w1_hi = sb("w1_hi", [128, len(FCH), 2, 128], F32R)
        w1_lo = sb("w1_lo", [128, len(FCH), 2, 128], F32R)
        w2 = sb("w2", [128, len(FCH), D])
        rot = sb("rot", [128, 4, S])
        tab = sb("tab", [128, 2, 2, 2, S])
        xs_hi = sb("xs_hi", [128, 2, S], F32R)
        xs_lo = sb("xs_lo", [128, 2, S], F32R)
        turned = sb("turned", [128, 2, S])
        squares = sb("squares", [128, 2, 2, S])
        rotated = sb("rotated", [128, RING, 2, 2, S])
        qr = sb("qr", [128, 2, S])
        qbd = sb("qbd", [128, 2, 2, NW, HPG, WIN])
        probs = sb("probs", [128, NW, 2 * WIN])
        pt = sb("pt", [128, 4, 2, 2, 64])
        vring = sb("vring", [128, RING, 4, 256])
        ot = sb("ot", [128, RING, 2, S])
        f_xc = sb("f_xc", [128, S])
        f_hi = sb("f_hi", [128, S], F32R)
        f_lo = sb("f_lo", [128, S], F32R)
        hid = sb("hid", [128, len(FCH), 2, S])
        f_sq = hid[:, 0, 0, :]
        wmask = sb("wmask", [128, 512], BF16)
        ident = sb("ident", [128, 128])
        ident_b = sb("ident_b", [128, 128], BF16)
        sel = sb("sel", [128, SEL])
        mean = sb("mean", [128, 128])
        norm = sb("norm", [96, S])
        nt_y = sb("nt_y", [96, S])
        nt_t = sb("nt_t", [96, S])
        r_rows = sb("r_rows", [96, S], BF16)
        r_sel = sb("r_sel", [96, 2 * G, 128], BF16)
        lv = sb("lv", [128, 3, TPB])
        rl_parts = sb("rl_parts", [128, 3, TPB], BF16)
        top = sb("top", [128, NW])
        total = sb("total", [128, 2, NW])
        vecs_all = sb("vecs_all", [128, DEPTH, 9])
        vecs = sb("vecs", [128, 9])
        qks_all = sb("qks_all", [128, DEPTH, 4])
        qks = sb("qks", [128, 4])

        def flat(t, pattern):
            return t[:].rearrange(pattern)
        rot_flat = flat(rotated, "p a b c d -> p (a b c d)")
        x_tok = rot_flat[:, 0:NT * D].rearrange("p (t d) -> p t d", d=D)
        xc_tok = rot_flat[:, NT * D:2 * NT * D].rearrange("p (t d) -> p t d", d=D)
        v_flat = flat(vring, "p a b c -> p (a b c)")
        sq_tok = v_flat[:, 0:NT * D].rearrange("p (t d) -> p t d", d=D)
        x1_back = sq_tok
        cmask = v_flat[:, NT * D:NT * D + 4 * S].rearrange("p (a t k) -> p a t k", a=2, t=TPB)
        ot_flat = flat(ot, "p a b c -> p (a b c)")
        x_fin = ot_flat[:, 2048:2304]
        st = ot_flat[:, 2304:2432].rearrange("p (k t) -> p k t", k=4)
        wqk_t = ot_flat[:, 2432:2464].rearrange("p (s e) -> p s e", s=2)
        bqk = ot_flat[0:E, 2464:2466]
        sets = []
        for r, room in enumerate((ot_flat[:, 0:2048], v_flat[:, NT * D + 4 * S:NT * D + 4 * S + 2048])):
            one = type("Set", (), {})
            one.xl = room[:, 0:256].rearrange("p (t d) -> p t d", d=D)
            one.xl_t = room[:, 256:512]
            one.qk = room[0:E, 512:1024].rearrange("p (s t) -> p s t", s=2)
            one.sc = room[:, 1024:1536].rearrange("p (t k) -> p t k", t=TPB)
            one.pt = room[:, 1536:2048].rearrange("p (k q) -> p k q", k=TPB)
            one.mx, one.sum, one.rec = (ot_flat[:, 2466 + TPB * k:2468 + TPB * k] for k in range(3 * r, 3 * r + 3))
            one.b_x, one.b_qk, one.b_sc, one.b_pt = ps[4 * r:4 * r + 4]
            sets.append(one)
        xl = sets[0].xl
        r_sel_f = raw[0:96, 0:2 * G * 128].rearrange("p (a x) -> p a x", a=2 * G)
        wmask_f = hid[:].rearrange("p a v b -> p (a v b)")[:, 0:512]
        w1_raw = hid[:].rearrange("p a v b -> p (a v b)")[:, 0:2 * FF]

        names = """loads wload rest_load wo_load cload x_load x1_saved x1_loaded out_done
            xs_ready qk_done rot_done sq_done added v_done v_out v_pad v_spread n_done n_copied newton  r_done r_used
            spread s_done top_done centred exp_done summed total_done scaled t_done t_out pv_done o_out
            f_done f_free fx_ready fsq_ready fc_ready lnewton  fn_ready fn_hi fn_lo gelu_done hid_ready
            hi_ready lo_ready w1hi_ready w1lo_ready tab_ready vec_ready zeroed consts stats a_dve a_step
            a_xl a_tr a_trc a_qk a_qkc a_sc a_masked a_max a_exp a_rec a_ptr a_ptc a_av a_x1 y_tr y_out
            sq_summed fin_copy fin_tr fin_add pool_zero mask_ready one_step m_step""".split()
        q = {n: sem(n) for n in names}
        W = type("Sems", (), q)

        rb = p_rb[:]
        rb2 = rb.rearrange("p (s t) -> p s t", s=2)
        rbb = rb.bitcast(BF16)

        block = ctx.enter_context(nc.Block())

        @block.sync
        def _(sp):
            for c in range(4):
                sp.dma_start(x_tok[:, 8 * c:8 * c + 8, :],
                             a["L0_attn_x"].rearrange("b (t p) d -> p (b t) d", p=128)[:, 8 * c:8 * c + 8, :]
                             ).then_inc(W.x_load, 16)
            sp.dma_start(ident[:], a["ident"]).then_inc(W.cload, 16)
            sp.dma_start(sel[:], a["sel"]).then_inc(W.cload, 16)
            sp.dma_start(mean[:], a["mean"]).then_inc(W.cload, 16)
            sp.dma_start(r_sel_f, a["spread"]).then_inc(W.cload, 16)
            sp.dma_start(wmask_f, a["wmask"]).then_inc(W.cload, 16)
            sp.dma_start(rot[:], a["rot"]).then_inc(W.cload, 16)
            sp.dma_start(cmask, a["cmask"]).then_inc(W.cload, 16)
            sp.dma_start(wqk_t, a["wqk_t"]).then_inc(W.cload, 16)
            sp.dma_start(bqk, a["bqk"]).then_inc(W.cload, 16)
            sp.dma_start(qks_all[:], a["qks"]).then_inc(W.cload, 16)
            sp.dma_start(vecs_all[:], a["vecs"]).then_inc(W.cload, 16)
            def load_rest(layer):
                sp.dma_start(w1_raw, a["L0_ffn_W1"][layer]).then_inc(W.rest_load, 16)
                sp.dma_start(w2[:, 0:2, :], a["L0_ffn_W2"][layer, 0:256, :].rearrange("(c p) d -> p c d", p=128)
                             ).then_inc(W.rest_load, 16)
                sp.dma_start(w2[0:FCH[2], 2, :], a["L0_ffn_W2"][layer, 256:FF, :]).then_inc(W.rest_load, 16)

            def load_wo(layer):
                sp.dma_start(wo[:], a["L0_ffn_Wo"][layer].rearrange("(c p) d -> p c d", p=128)
                             ).then_inc(W.wo_load, 16)

            load_wo(0)
            sp.wait_ge(W.mask_ready, 2)
            sp.dma_start(raw[:], a["L0_ffn_Wqkv"][0]).then_inc(W.wload, 16)
            load_rest(0)
            sp.wait_ge(W.a_x1, 2 * B)
            sp.dma_start(x1_dram, x_tok).then_inc(W.x1_saved, 16)
            sp.wait_ge(W.lo_ready, G)
            sp.dma_start(raw[:], a["L0_ffn_Wqkv"][1]).then_inc(W.wload, 16)
            sp.wait_ge(W.zeroed, 1)

            def clocks(n0, lo_c, hi_c, projects=True):
                for c in range(lo_c, hi_c):
                    n = n0 + c
                    if projects and live(n):
                        wait_apart(sp, W.v_out, n + 1, W.zeroed)
                        wait_apart(sp, W.v_spread, n * 32, W.zeroed)
                        sp.dma_start(vring[WIN:, c % RING, 0::2, :], vring[0:128 - WIN, c % RING, 1::2, :]
                                     ).then_inc(W.v_spread, 16)
                        sp.dma_start(vring[0:WIN, c % RING, 2, :], vring[128 - WIN:, c % RING, 1, :]
                                     ).then_inc(W.v_spread, 16)
                    m = n - LAG_R
                    if not live(m):
                        continue
                    wait_apart(sp, W.r_used, m * 2 + 1, W.zeroed)
                    wait_apart(sp, W.s_done, m - 1, W.zeroed)
                    wait_apart(sp, W.spread, m * 64, W.zeroed)
                    for j in range(HPG):
                        rows = slice(HALF * j, HALF * (j + 1))
                        sp.dma_start(qbd[rows, c % 2, :, :, j, :],
                                     qr[rows, :, :].rearrange("p x (w t) -> p x w t", w=NW)).then_inc(W.spread, 16)

            clocks(0, 0, RING)
            clocks(RING, 0, RING)
            with sp.Fori(0, DEPTH - 1) as layer:
                nl, il = layer * (PAIRS * RING), layer * B
                with sp.Fori(2, PAIRS) as p:
                    clocks(nl + p * RING, 0, RING)
                for j in range(2):
                    n0 = nl + (PAIRS + j) * RING
                    if j == 0:
                        clocks(n0, 0, RING)
                        continue
                    clocks(n0, 0, 6)
                    wait_apart(sp, W.f_done, (il + (B - 1)) * FU + 1, W.zeroed)
                    load_wo(layer + 1)
                    clocks(n0, 6, RING)
                wait_apart(sp, W.f_free, (il + B) * FU + 1, W.zeroed)
                load_rest(layer + 1)
                wait_apart(sp, W.lo_ready, (layer + 2) * G, W.zeroed)
                nxt = (layer + 2) % DEPTH
                sp.dma_start(raw[:], a["L0_ffn_Wqkv"][nxt]).then_inc(W.wload, 16)
            with sp.Fori(2, PAIRS) as p:
                clocks(p * RING + (DEPTH - 1) * PAIRS * RING, 0, RING)
            clocks(CLOCKS, 0, RING, False)
            sp.wait_ge(W.pv_done, 2 * CLOCKS)
            sp.wait_ge(W.x1_saved, 16)
            sp.dma_start(x1_back, x1_dram).then_inc(W.x1_loaded, 16)
            out_v = out.rearrange("b (t p) d -> p b t d", p=128)
            with sp.Fori(0, B) as b:
                wait_apart(sp, W.fin_add, b + 1 + 1, W.zeroed)
                sp.dma_start(out_v[:, b, :, :], x1_back.rearrange("p (b t) d -> p b t d", t=TPB)[:, b, :, :]
                             ).then_inc(W.out_done, 16)
            sp.wait_ge(W.wload, 16 * (DEPTH + 1))
            sp.wait_ge(W.out_done, 16 * B)

        @block.tensor
        def _(pe):
            mm = nc.tensor.matmul

            def split3(dst, w_hi, w_lo, x_hi, x_lo):
                mm(dst, w_lo, x_hi, start=True, stop=False)
                mm(dst, w_hi, x_lo, start=False, stop=False)
                return mm(dst, w_hi, x_hi, start=False, stop=True)

            pe.wait_ge(W.cload, 16 * CLOADS)
            with pe.Fori(0, B // 2) as j:
                for r, k_ in enumerate(sets):
                    pe.wait_ge(W.a_xl, j * 2 + r + 1)
                    for t in range(TPB):
                        ins = nc.tensor.transpose(k_.b_x[:, 128 * t:128 * t + 128], k_.xl[:, t, :], ident[:])
                    ins.then_inc(W.a_tr, 1)
                for r, k_ in enumerate(sets):
                    pe.wait_ge(W.a_trc, j * 2 + r + 1)
                    for s in range(2):
                        ins = mm(k_.b_qk[0:E, 256 * s:256 * s + 256], wqk_t[:, s, :], k_.xl_t, start=True, stop=True)
                    ins.then_inc(W.a_qk, 1)
                for r, k_ in enumerate(sets):
                    pe.wait_ge(W.a_qkc, j * 4 + 2 * r + 2)
                    for t in range(TPB):
                        ins = mm(k_.b_sc[:, 256 * t:256 * t + 256], k_.qk[:, 0, 128 * t:128 * t + 128],
                                 k_.qk[:, 1, :], start=True, stop=True)
                    ins.then_inc(W.a_sc, 1)
                for r, k_ in enumerate(sets):
                    pe.wait_ge(W.a_exp, j * 4 + 2 * r + 2)
                    for k in range(TPB):
                        for t in range(TPB):
                            ins = nc.tensor.transpose(k_.b_pt[:, 256 * k + 128 * t:256 * k + 128 * t + 128],
                                                      k_.sc[:, t, 128 * k:128 * k + 128], ident[:])
                    ins.then_inc(W.a_ptr, 1)
                for r, k_ in enumerate(sets):
                    pe.wait_ge(W.a_ptc, j * 2 + r + 1)
                    for t in range(TPB):
                        for k in range(TPB):
                            ins = mm(k_.b_x[:, 128 * t:128 * t + 128], k_.pt[:, k, 128 * t:128 * t + 128],
                                     k_.xl[:, k, :], start=(k == 0), stop=(k == TPB - 1))
                    ins.then_inc(W.a_av, 1)
            with pe.Fori(0, B) as b:
                pe.wait_ge(W.a_xl, b + (B + 1))
                for t in range(TPB):
                    ins = nc.tensor.transpose(ps[0][:, 128 * t:128 * t + 128], xl[:, t, :], ident[:])
                ins.then_inc(W.y_tr, 1)
                pe.wait_ge(W.y_out, b + 1)

            pe.wait_ge(W.consts, 1)
            pe.wait_ge(W.v_pad, 1)
            pe.wait_ge(W.mask_ready, 2)
            pe.wait_ge(W.lo_ready, G)
            pe.wait_ge(W.zeroed, 1)

            def body(n0, i0, s1, s3):
                for c in range(RING):
                    n, g, h = n0 + c, c % G, c // G
                    i = i0 + h
                    proj = live(n) and s1 is not None
                    fb = i - LAG_F
                    units = fb * FU + 2 * g

                    def attend(hp):
                        m = n - LAG_PV
                        if not live(m):
                            return
                        if hp == 0:
                            wait(pe, W.t_out, m * 2 + 2)
                            wait(pe, W.v_spread, m * 32 + 32)
                        wait(pe, W.o_out, m * 4 - 2 + 2 * hp)
                        o_w = p_o[hp][:].rearrange("p (a e t x) -> p a e t x", a=2, e=2, t=2)
                        for t in range(4):
                            ins = mm(o_w[:, t // 2, :, t % 2, :], vring[:, c, t, 128 * hp:128 * hp + 128],
                                     pt[:, t, hp, :, :], start=True, stop=True)
                        ins.then_inc(W.pv_done, 1)

                    def project(s):
                        wait(pe, W.rot_done, n * 4 - 2 + 2 * s)
                        xh, xl_ = xs_hi[:, h, :], xs_lo[:, h, :]
                        for half in range(2):
                            ins = split3(p_qk[s][:, S * half:S * half + S], qk_hi[:, g, s, half, :],
                                         qk_lo[:, g, s, half, :], xh, xl_)
                        ins.then_inc(W.qk_done, 1)

                    def values():
                        wait(pe, W.v_out, n)
                        if s3 is not None:
                            wait(pe, W.f_free, units + 1)
                        for t in range(TPB):
                            toks = slice(128 * t, 128 * t + 128)
                            ins = split3(p_v[:, 256 * t:256 * t + 256], xs_hi[:, h, toks],
                                         xs_lo[:, h, toks], v_hi[:, g, :], v_lo[:, g, :])
                        ins.then_inc(W.v_done, 1)

                    def feed(late):
                        u, fbank = 2 * g + late, (p_v if late else p_rb)[:]
                        wait(pe, W.f_free, fb * FU + u + 1)
                        if u == 0:
                            wait(pe, W.o_out, fb * (4 * G) + 4 * G)
                            if g == 0:
                                wait(pe, W.wo_load, wo_count)
                            for k in range(2 * G):
                                ins = mm(fbank[:, 0:S], wo[:, k, :], ot[:, G * h + k // 2, k % 2, :],
                                         start=(k == 0), stop=(k == 2 * G - 1))
                        elif u == 1:
                            wait(pe, W.fx_ready, fb * 2 + 2)
                            ins = mm(fbank[:, 0:S], mean[:], f_xc[:], start=True, stop=True)
                        elif u == 2:
                            wait(pe, W.fsq_ready, fb + 1)
                            for t in range(TPB):
                                ins = mm(fbank[:, t:t + 1], f_sq[:, 128 * t:128 * t + 128], mean[:, 0:1],
                                         start=True, stop=True)
                        elif u == 3:
                            wait(pe, W.lnewton, fb * NEWTON + NEWTON)
                            for t in range(TPB):
                                for k in range(3):
                                    ins = mm(fbank[:, 128 * t:128 * t + 128],
                                             rl_parts[:, k, t:t + 1].to_broadcast([128, 128]),
                                             ident_b[:], start=(k == 0), stop=(k == 2))
                        elif u < 7:
                            k = u - 4
                            wait(pe, W.fn_lo, fb + 1)
                            if k == 0:
                                wait(pe, W.w1lo_ready, w1_count)
                            for v in range(2):
                                ins = split3(fbank[0:FCH[k], S * v:S * v + S], w1_hi[:, k, v, 0:FCH[k]],
                                             w1_lo[:, k, v, 0:FCH[k]], f_hi[:], f_lo[:])
                        else:
                            wait(pe, W.hid_ready, fb * 3 + 3)
                            for k, w in enumerate(FCH):
                                ins = mm(fbank[:, 0:S], w2[0:w, k, :], hid[0:w, k, 1, :], start=(k == 0), stop=(k == 2))
                        ins.then_inc(W.f_done, 1)

                    attend(0)
                    m = n - LAG_R
                    if live(m):
                        if live(n - 1):
                            wait(pe, W.n_copied, n)
                        else:
                            wait(pe, W.f_free, units)
                        if g == 1:
                            wait(pe, W.newton, i * ROOT)
                        for s in range(2):
                            ins = mm(rb2[:, s, :], r_sel[:, s * G + (g - LAG_R) % G, :], r_rows[:],
                                     start=True, stop=True)
                        ins.then_inc(W.r_done, 1)
                    if proj:
                        if g == 0:
                            wait(pe, W.xs_ready, i * 2 + 2)
                        project(0)
                    attend(1)
                    if proj:
                        values()
                        project(1)
                    if s3 is not None:
                        if live(n - LAG_R):
                            wait(pe, W.r_used, (n - LAG_R) * 2 + 2)
                        feed(0)
                    m = n - LAG_T
                    if live(m):
                        wait(pe, W.scaled, m + 1)
                        wait(pe, W.t_out, m * 2)
                        pm = probs[:].rearrange("p w k -> p (w k)")
                        for t in range(4):
                            ins = nc.tensor.transpose(p_t[:, 128 * t:128 * t + 128], pm[:, 128 * t:128 * t + 128],
                                                      ident[:])
                        ins.then_inc(W.t_done, 1)
                    m = n - LAG_S
                    if live(m):
                        wait(pe, W.centred, m)
                        wait(pe, W.r_used, m * 2 + 2)
                        wait(pe, W.spread, m * 64 + 64)
                        slot_k, slot_q = (c - LAG_S) % RING, (c - LAG_S + LAG_R) % 2
                        ins = mm(p_s[:], ident_b[:], wmask[:], start=True, stop=False, skip_group_check=True)
                        for w in range(NW):
                            lo = max(0, w - 1) * WIN
                            hi = (w + 1) * WIN
                            end = 2 * WIN * (ORDER.index(w) + 1)
                            dst = p_s[:, end - (hi - lo):end]
                            for half in range(2):
                                ins = mm(dst, qbd[:, slot_q, half, w, :, :].rearrange("p j t -> p (j t)"),
                                         rotated[:, slot_k, 1, half, lo:hi], start=False,
                                         stop=(w == NW - 1 and half == 1), skip_group_check=True)
                        ins.then_inc(W.s_done, 1)
                    if proj:
                        wait(pe, W.sq_summed, n + 1)
                        if s3 is not None:
                            wait(pe, W.f_free, units + 1 + 1)
                        else:
                            wait(pe, W.n_copied, n)
                            wait(pe, W.r_used, (n - LAG_R) * 2 + 2)
                        for s in range(2):
                            at = 32 - HPG - (s * HEADS + HPG * g)
                            ins = mm(rb[0:96, 0:S], sel[:, at:at + 96], squares[:, s, 0, :],
                                     start=(s == 0), stop=(s == 1))
                        ins.then_inc(W.n_done, 1)
                    if s3 is not None:
                        if proj:
                            wait(pe, W.v_out, n + 1)
                        feed(1)

            wo_count, w1_count = 16, 1

            def reload_projection(layer):
                wait_apart(pe, W.lo_ready, (layer + 2) * G, W.zeroed)

            def reload_rest(layer):
                wait_apart(pe, W.wo_load, (layer + 2) * 16, W.zeroed)
                wait_apart(pe, W.rest_load, (layer + 2) * 48, W.zeroed)
                wait_apart(pe, W.w1lo_ready, layer + 2, W.zeroed)

            pe.wait_ge(W.wo_load, 16)
            pe.wait_ge(W.rest_load, 48)
            schedule(pe, body, reload_projection, reload_rest)

            with pe.Fori(0, B) as b:
                pe.wait_ge(W.fin_copy, b + 1)
                wait(pe, W.fin_add, b + 1)
                for t in range(TPB):
                    ins = nc.tensor.transpose(ps[0][:, 128 * t:128 * t + 128], x_fin[:, 128 * t:128 * t + 128],
                                              ident[:])
                ins.then_inc(W.fin_tr, 1)

        @block.vector
        def _(dve):
            v = nc.vector

            def inverse_root(s, y, t, parts, done, base):
                step = [0]

                def link(ins):
                    step[0] += 1
                    ins.then_inc(done, 1)
                    dve.wait_ge(done, base + step[0])
                link(v.tensor_scalar(y.bitcast(I32), s.bitcast(I32), -0.5, MAGIC, ALU.mult, ALU.add))
                for _ in range(3):
                    link(v.tensor_tensor(t, y, y, ALU.mult))
                    link(v.scalar_tensor_tensor(t, t, -0.5, s, ALU.mult, ALU.mult))
                    link(v.scalar_tensor_tensor(y, t, 1.5, y, ALU.add, ALU.mult))
                if parts is not None:
                    link(v.tensor_copy(parts[0], y))
                    link(v.tensor_tensor(t, y, parts[0], ALU.subtract))
                    link(v.tensor_copy(parts[1], t))
                    link(v.tensor_tensor(parts[2], t, parts[1], ALU.subtract))

            dve.wait_ge(W.cload, 16 * CLOADS)
            v.tensor_copy(r_sel[:], r_sel_f).then_inc(W.mask_ready, 1)
            v.tensor_copy(ident_b[:], ident[:]).then_inc(W.consts, 1)
            v.tensor_copy(wmask[:], wmask_f).then_inc(W.mask_ready, 1)

            def layer_norm(k):
                base = 3 * k
                v.tensor_reduce(st[:, 0, :], x_tok, AX.X, ALU.add).then_inc(W.stats, 1)
                dve.wait_ge(W.stats, base + 1)
                v.tensor_scalar(st[:, 0, :], st[:, 0, :], 1.0 / D, None, ALU.mult).then_inc(W.stats, 1)
                dve.wait_ge(W.stats, base + 2)
                v.tensor_tensor(xc_tok, x_tok, st[:, 0, :].unsqueeze(2).to_broadcast([128, NT, D]),
                                ALU.subtract).then_inc(W.a_dve, 1)
                dve.wait_ge(W.a_step, k + 1)
                v.tensor_reduce(st[:, 1, :], sq_tok, AX.X, ALU.add).then_inc(W.stats, 1)
                dve.wait_ge(W.stats, base + 3)
                v.tensor_scalar(st[:, 1, :], st[:, 1, :], 1.0 / D, LN_EPS, ALU.mult, ALU.add).then_inc(W.one_step, 1)
                dve.wait_ge(W.one_step, k + 1)
                inverse_root(st[:, 1, :], st[:, 2, :], st[:, 3, :], None, W.m_step, 10 * k)

            def normed(b, to):
                return v.tensor_tensor(to, xc_tok.rearrange("p (b t) d -> p b t d", t=TPB)[:, b, :, :],
                                       st[:, 2, :].rearrange("p (b t) -> p b t", t=TPB)[:, b, :]
                                       .unsqueeze(2).to_broadcast([128, TPB, D]), ALU.mult)

            for c in range(4):
                dve.wait_ge(W.x_load, 64)
            layer_norm(0)
            x_b = x_tok.rearrange("p (b t) d -> p b t d", t=TPB)
            with dve.Fori(0, B // 2) as j:
                for r, k_ in enumerate(sets):
                    dve.wait_ge(W.a_av, j * 2 + r + 1)
                    normed(j * 2 + r, k_.xl).then_inc(W.a_xl, 1)
                for r, k_ in enumerate(sets):
                    dve.wait_ge(W.a_sc, j * 2 + r + 1)
                    ps2 = k_.b_sc[:].rearrange("p (t k) -> p t k", t=TPB)
                    v.tensor_tensor(k_.sc, ps2, cmask[:, 0, :, :], ALU.mult).then_inc(W.a_masked, 1)
                    dve.wait_ge(W.a_masked, j * 4 + 2 * r + 1)
                    v.tensor_tensor(k_.sc, k_.sc, cmask[:, 1, :, :], ALU.add).then_inc(W.a_masked, 1)
                    dve.wait_ge(W.a_masked, j * 4 + 2 * r + 2)
                    v.tensor_reduce(k_.mx, k_.sc, AX.X, ALU.max, negate=True).then_inc(W.a_max, 1)
                for r, k_ in enumerate(sets):
                    dve.wait_ge(W.a_exp, j * 4 + 2 * r + 2)
                    v.reciprocal(k_.rec, k_.sum).then_inc(W.a_rec, 1)
                for r, k_ in enumerate(sets):
                    dve.wait_ge(W.a_rec, j * 2 + r + 1)
                    dve.wait_ge(W.a_av, j * 2 + r + 1 + 2)
                    for t in range(TPB):
                        xt = x_b[:, j * 2 + r, t, :]
                        v.scalar_tensor_tensor(xt, k_.b_x[:, 128 * t:128 * t + 128], k_.rec[:, t:t + 1], xt,
                                               ALU.mult, ALU.add).then_inc(W.a_x1, 1)
            dve.wait_ge(W.a_x1, 2 * B)
            layer_norm(1)
            with dve.Fori(0, B) as b:
                wait(dve, W.y_tr, b + 1)
                normed(b, xl).then_inc(W.a_xl, 1)

            def split_projection(count):
                for g in range(G):
                    dve.wait_ge(W.hi_ready, count * (3 * G) + 3 * g + 3)
                    for s in range(2):
                        src = raw[:, INNER * s + 256 * g:INNER * s + 256 * g + 256].rearrange(
                            "p (h x f) -> p x h f", h=HPG, x=2)
                        hi = qk_hi[:, g, s, :, :].bitcast(F32).rearrange("p x (h f) -> p x h f", h=HPG)
                        lo = qk_lo[:, g, s, :, :].rearrange("p x (h f) -> p x h f", h=HPG)
                        v.tensor_tensor(lo, src, hi, ALU.subtract)
                    v.tensor_tensor(v_lo[:, g, :], raw[:, 2 * INNER + 256 * g:2 * INNER + 256 * g + 256],
                                    v_hi[:, g, :].bitcast(F32), ALU.subtract).then_inc(W.lo_ready, 1)

            def tables(layer, count):
                v.tensor_copy(qks[:], qks_all[:, layer, :]).then_inc(W.tab_ready, 1)
                dve.wait_ge(W.tab_ready, count * 9 + 1)
                for s in range(2):
                    for half in range(2):
                        v.tensor_scalar(tab[:, s, 0, half, :], rot[:, 2 * s, :], qks[:, 2 * s + half:2 * s + half + 1],
                                        None, ALU.mult).then_inc(W.tab_ready, 1)
                        v.tensor_scalar(tab[:, s, 1, half, :], rot[:, 2 * s + 1, :],
                                        qks[:, 2 * s + 1 - half:2 * s + 2 - half], -1.0 if half == 0 else 1.0,
                                        ALU.mult, ALU.mult).then_inc(W.tab_ready, 1)
                wait_apart(dve, W.tab_ready, count * 9 + 9, W.zeroed)

            def split_w1(count):
                dve.wait_ge(W.w1hi_ready, count * 6 + 6)
                for k, w in enumerate(FCH):
                    for g in range(2):
                        off = (FF if g == 0 else 0) + 128 * k
                        ins = v.tensor_tensor(w1_lo[:, k, g, 0:w], w1_raw[:, off:off + w],
                                              w1_hi[:, k, g, 0:w].bitcast(F32), ALU.subtract)
                ins.then_inc(W.w1lo_ready, 1)

            def vectors(layer, count):
                v.tensor_copy(vecs[:], vecs_all[:, layer, :]).then_inc(W.vec_ready, 1)
                wait_apart(dve, W.vec_ready, count + 1, W.zeroed)

            def shift_rest(batch, h, count):
                wait(dve, W.fc_ready, count * 2 + 2)
                for lo in (0, 64):
                    rows = slice(lo, lo + 64)
                    off = 1 - lo // 64
                    v.tensor_tensor(xs_lo[rows, h, :], X[rows, batch, off:off + S],
                                    xs_hi[rows, h, :].bitcast(F32), ALU.subtract).then_inc(W.xs_ready, 1)

            split_projection(0)
            tables(0, 0)
            split_w1(0)
            vectors(0, 0)
            dve.wait_ge(W.x1_saved, 16)
            dve.wait_ge(W.zeroed, 1)
            dve.wait_ge(W.y_out, B)
            shift_rest(0, 0, 0)

            def body(n0, i0, s1, s3):
                for c in range(RING):
                    n, g, h = n0 + c, c % G, c // G
                    i = i0 + h
                    proj = live(n) and s1 is not None
                    fb = i - LAG_F

                    def turn(s):
                        wait(dve, W.sq_done, n * 2 + 1 + s)
                        wait(dve, W.added, n * 2 + s)
                        if s == 1:
                            wait(dve, W.s_done, n - RING + 1)
                        src = p_qk[s][:].rearrange("p (x t) -> p x t", x=2)
                        v.tensor_tensor(rotated[:, c, s, :, :], src, tab[:, s, 0, :, :], ALU.mult
                                        ).then_inc(W.rot_done, 1)
                        v.tensor_tensor(turned[:], src[:, ::-1, :], tab[:, s, 1, :, :], ALU.mult
                                        ).then_inc(W.rot_done, 1)

                    def feed(late):
                        u, fbank = 2 * g + late, (p_v if late else p_rb)[:]
                        pair = s3 * 2 + h
                        wait(dve, W.f_done, fb * FU + u + 1)
                        xb = X[:, pair, 1:S + 1]
                        if u == 0:
                            v.tensor_tensor(xb, fbank[:, 0:S], xb, ALU.add).then_inc(W.f_free, 1)
                        elif u == 1:
                            v.tensor_tensor(f_xc[:], f_xc[:], fbank[:, 0:S], ALU.subtract).then_inc(W.f_free, 1)
                        elif u == 2:
                            v.tensor_scalar(lv[:, 0, :], fbank[:, 0:TPB], LN_EPS, None, ALU.add).then_inc(W.f_free, 1)
                            dve.wait_ge(W.f_free, fb * FU + 3 + 1)
                            inverse_root(lv[:, 0, :], lv[:, 1, :], lv[:, 2, :],
                                         [rl_parts[:, k, :] for k in range(3)], W.lnewton, fb * NEWTON)
                        elif u == 3:
                            v.tensor_tensor(f_xc[:], f_xc[:], fbank[:, 0:S], ALU.mult).then_inc(W.f_free, 1)
                            dve.wait_ge(W.f_free, fb * FU + 4 + 1)
                            v.tensor_scalar(f_xc[:], f_xc[:], vecs[:, 0:1], vecs[:, 1:2], ALU.mult, ALU.add
                                            ).then_inc(W.fn_ready, 1)
                        elif u < 7:
                            k = u - 4
                            w = FCH[k]
                            v.tensor_copy(hid[0:w, k, :, :], fbank[0:w, :].rearrange("p (v t) -> p v t", v=2)
                                          ).then_inc(W.f_free, 1)
                        else:
                            v.scalar_tensor_tensor(xb, fbank[:, 0:S], vecs[:, 2:3], xb, ALU.add, ALU.add
                                                   ).then_inc(W.f_free, 1)

                    def gate(first, last):
                        for k in range(first, last):
                            w = FCH[k]
                            wait(dve, W.gelu_done, fb * 3 + k + 1)
                            v.scalar_tensor_tensor(hid[0:w, k, 1, :], hid[0:w, k, 1, :], vecs[0:w, 6 + k:7 + k],
                                                   hid[0:w, k, 0, :], ALU.add, ALU.mult).then_inc(W.hid_ready, 1)

                    def root(first, last):
                        if g != 0 or not live(n - 1):
                            return
                        for k in range(first, last):
                            if k == 0:
                                wait(dve, W.n_copied, n)
                                ins = v.tensor_scalar(norm[:], norm[:], 1e-24, None, ALU.max)
                            elif k == 1:
                                ins = v.tensor_scalar(nt_y[:].bitcast(I32), norm[:].bitcast(I32), -0.5, MAGIC,
                                                      ALU.mult, ALU.add)
                            elif k < 11 and k % 3 == 2:
                                ins = v.tensor_tensor(nt_t[:], nt_y[:], nt_y[:], ALU.mult)
                            elif k < 11 and k % 3 == 0:
                                ins = v.scalar_tensor_tensor(nt_t[:], nt_t[:], -0.5, norm[:], ALU.mult, ALU.mult)
                            elif k < 11:
                                ins = v.scalar_tensor_tensor(nt_y[:], nt_t[:], 1.5, nt_y[:], ALU.add, ALU.mult)
                            elif k == 11:
                                ins = v.tensor_copy(r_rows[:], nt_y[:])
                            elif k == 12:
                                ins = v.tensor_tensor(nt_t[:], nt_y[:], r_rows[:], ALU.subtract)
                            elif k == 13:
                                v.tensor_copy(r_rows[32:64, :], nt_t[32:64, :])
                                ins = v.tensor_copy(r_rows[64:96, :], nt_t[64:96, :])
                            else:
                                ins = v.tensor_tensor(r_rows[64:96, :], nt_t[64:96, :], r_rows[64:96, :],
                                                      ALU.subtract)
                            ins.then_inc(W.newton, 1)
                            if k < ROOT - 1:
                                dve.wait_ge(W.newton, (i - 1) * ROOT + k + 1)

                    m = n - LAG_T
                    if live(m):
                        wait(dve, W.exp_done, m + 1)
                        v.tensor_reduce(total[:, 0, :], probs[:], AX.X, ALU.add).then_inc(W.summed, 1)
                        wait(dve, W.summed, m + 1)
                        wait(dve, W.scaled, m)
                        v.reciprocal(total[:, 1, :], total[:, 0, :]).then_inc(W.total_done, 1)
                    m = n - LAG_R
                    if live(m):
                        slot = (c - LAG_R) % RING
                        wait(dve, W.r_done, m + 1)
                        wait(dve, W.added, m * 2 + 2)
                        wait(dve, W.spread, m * 64)
                        for s in range(2):
                            src = rotated[:, slot, s, :, :]
                            v.tensor_tensor(qr[:] if s == 0 else src, src,
                                            rb2[:, s, :].unsqueeze(1).to_broadcast([128, 2, S]), ALU.mult
                                            ).then_inc(W.r_used, 1)
                    root(0, 5)
                    if proj:
                        turn(0)
                    root(5, 9)
                    if s3 is not None:
                        if g == G - 1:
                            gate(0, 2)
                        feed(0)
                    root(9, 12)
                    if proj:
                        turn(1)
                    root(12, ROOT)
                    if s3 is not None and g == G - 1:
                        gate(2, 3)
                    m = n - LAG_S
                    if live(m):
                        wait(dve, W.s_done, m + 1)
                        sc3 = p_s[:].rearrange("p (w k) -> p w k", w=NW)
                        v.tensor_reduce(top[:], sc3, AX.X, ALU.max).then_inc(W.top_done, 1)
                        wait(dve, W.top_done, m + 1)
                        wait(dve, W.t_done, m)
                        v.tensor_tensor(probs[:], sc3,
                                        top[:].unsqueeze(2).to_broadcast([128, NW, 2 * WIN]), ALU.subtract
                                        ).then_inc(W.centred, 1)
                    if proj:
                        wait(dve, W.n_done, n + 1)
                        if g == 0:
                            if live(n - 1):
                                wait(dve, W.newton, i * ROOT)
                            v.tensor_copy(norm[:], rb[0:96, 0:S]).then_inc(W.n_copied, 1)
                        else:
                            v.tensor_tensor(norm[:], rb[0:96, 0:S], norm[:], ALU.add).then_inc(W.n_copied, 1)
                    if s3 is not None:
                        feed(1)
                    if proj and g == 2:
                        shift_rest(s1 * 2 + 1 if h == 0 else (s1 * 2 + 2) % B, 1 - h, i + 1)

            def reload_projection(layer):
                split_projection(layer + 1)
                tables(layer + 1, layer + 1)

            def reload_rest(layer):
                split_w1(layer + 1)
                vectors(layer + 1, layer + 1)

            schedule(dve, body, reload_projection, reload_rest)
            dve.wait_ge(W.x1_loaded, 16)
            xb1 = x1_back.rearrange("p (b t) d -> p b t d", t=TPB)
            with dve.Fori(0, B) as b:
                dve.wait_ge(W.fin_tr, b + 1 + 1)
                v.tensor_tensor(xb1[:, b, :, :], xb1[:, b, :, :],
                                ps[0][:, 0:S].rearrange("p (t d) -> p t d", t=TPB), ALU.add).then_inc(W.fin_add, 1)

        @block.scalar
        def _(act):
            A = nc.scalar.activation

            def copy(dst, src):
                return A(dst, src, ACT.Copy)

            def layer_norm(k):
                act.wait_ge(W.a_dve, k + 1)
                A(sq_tok, xc_tok, ACT.Square).then_inc(W.a_step, 1)

            layer_norm(0)
            act.wait_ge(W.cload, 16 * CLOADS)
            with act.Fori(0, B // 2) as j:
                for r, k_ in enumerate(sets):
                    act.wait_ge(W.a_tr, j * 2 + r + 1)
                    copy(k_.xl_t, k_.b_x[:, 0:S]).then_inc(W.a_trc, 1)
                for r, k_ in enumerate(sets):
                    act.wait_ge(W.a_qk, j * 2 + r + 1)
                    for s in range(2):
                        A(k_.qk[:, s, :], k_.b_qk[0:E, 256 * s:256 * s + 256], ACT.Identity, bias=bqk[:, s:s + 1]
                          ).then_inc(W.a_qkc, 1)
                for r, k_ in enumerate(sets):
                    act.wait_ge(W.a_max, j * 2 + r + 1)
                    for t in range(TPB):
                        A(k_.sc[:, t, :], k_.sc[:, t, :], ACT.Exp, bias=k_.mx[:, t:t + 1],
                          accum_out=k_.sum[:, t:t + 1]).then_inc(W.a_exp, 1)
                for r, k_ in enumerate(sets):
                    act.wait_ge(W.a_ptr, j * 2 + r + 1)
                    copy(k_.pt, k_.b_pt[:].rearrange("p (k q) -> p k q", k=TPB)).then_inc(W.a_ptc, 1)
            layer_norm(1)
            act.wait_ge(W.zeroed, 1)
            with act.Fori(0, B) as b:
                act.wait_ge(W.y_tr, b + 1 + 1)
                copy(X[:, b, 1:S + 1], ps[0][:, 0:S]).then_inc(W.y_out, 1)

            def split_projection(count, done):
                act.wait_ge(W.wload, (count + 1) * 16)
                if done is not None:
                    act.wait_ge(W.v_done, done)
                for g in range(G):
                    for s in range(2):
                        src = raw[:, INNER * s + 256 * g:INNER * s + 256 * g + 256].rearrange(
                            "p (h x f) -> p x h f", h=HPG, x=2)
                        copy(qk_hi[:, g, s, :, :].rearrange("p x (h f) -> p x h f", h=HPG), src
                             ).then_inc(W.hi_ready, 1)
                    copy(v_hi[:, g, :], raw[:, 2 * INNER + 256 * g:2 * INNER + 256 * g + 256]).then_inc(W.hi_ready, 1)

            def shift_split(batch, h):
                for lo in (0, 64):
                    rows = slice(lo, lo + 64)
                    off = 1 - lo // 64
                    copy(xs_hi[rows, h, :], X[rows, batch, off:off + S]).then_inc(W.fc_ready, 1)

            def split_w1(count):
                act.wait_ge(W.rest_load, (count + 1) * 48)
                for k, w in enumerate(FCH):
                    for g in range(2):
                        off = (FF if g == 0 else 0) + 128 * k
                        copy(w1_hi[:, k, g, 0:w], w1_raw[:, off:off + w]).then_inc(W.w1hi_ready, 1)

            split_projection(0, None)
            split_w1(0)
            act.wait_ge(W.vec_ready, 1)
            act.wait_ge(W.y_out, B)
            shift_split(0, 0)

            def body(n0, i0, s1, s3):
                for c in range(RING):
                    n, g, h = n0 + c, c % G, c // G
                    i = i0 + h
                    proj = live(n) and s1 is not None
                    fb = i - LAG_F

                    def square(s):
                        wait(act, W.qk_done, n * 2 + 1 + s)
                        wait(act, W.n_done, n)
                        A(squares[:, s, :, :], p_qk[s][:].rearrange("p (x t) -> p x t", x=2), ACT.Square
                          ).then_inc(W.sq_done, 1)

                    def values():
                        wait(act, W.v_done, n + 1)
                        wait(act, W.pv_done, (n - RING) * 2 + 2)
                        copy(vring[:, c, 1::2, :], p_v[:].rearrange("p (t d) -> p t d", t=2)
                             ).then_inc(W.v_out, 1)

                    def feed(late):
                        u, fbank = 2 * g + late, (p_v if late else p_rb)[:]
                        if u == 1:
                            wait(act, W.f_free, fb * FU + 2 + 1)
                            A(f_sq, f_xc[:], ACT.Square).then_inc(W.fsq_ready, 1)

                    def gelu(k):
                        w = FCH[k]
                        wait(act, W.f_free, fb * FU + k + 5 + 1)
                        A(hid[0:w, k, 0, :], hid[0:w, k, 0, :], ACT.Gelu, bias=vecs[0:w, 3 + k:4 + k]
                          ).then_inc(W.gelu_done, 1)

                    if proj:
                        square(0)
                        values()
                    m = n - LAG_PV
                    if live(m):
                        wait(act, W.f_done, (i - 4) * FU + 1)
                        for hp in range(2):
                            wait(act, W.pv_done, m * 2 + 1 + hp)
                            for k in range(2):
                                rows = slice(64 * k, 64 * k + 64)
                                copy(ot[rows, c, hp, :].rearrange("p (w x) -> p w x", w=NW),
                                     p_o[hp][rows, :].rearrange("p (w x) -> p w x", w=NW)[
                                         :, :, WIN * k:WIN * k + WIN]).then_inc(W.o_out, 1)
                    if proj:
                        square(1)
                    if s3 is not None:
                        feed(0)
                    if s3 is not None and g == 0:
                        wait(act, W.f_free, fb * FU + 1 + 1)
                        for lo in (0, 64):
                            rows = slice(lo, lo + 64)
                            off = 1 - lo // 64
                            copy(f_xc[rows, :], X[rows, s3 * 2 + h, off:off + S]).then_inc(W.fx_ready, 1)
                    m = n - LAG_T
                    if live(m):
                        wait(act, W.t_done, m + 1)
                        wait(act, W.pv_done, m * 2)
                        for e in range(2):
                            rows = slice(64 * e, 64 * e + 64)
                            copy(pt[rows, :, :, e, :], p_t[rows, :].rearrange("p (t h x) -> p t h x", t=4, h=2)
                                 ).then_inc(W.t_out, 1)
                    if s3 is not None and g == G - 1:
                        gelu(2)
                    m = n - LAG_S
                    if live(m):
                        slot = (c - LAG_S) % 2
                        wait(act, W.centred, m + 1)
                        A(probs[:], probs[:], ACT.Exp).then_inc(W.exp_done, 1)
                    if proj:
                        if g == 1:
                            wait(act, W.f_free, (i - 4) * FU + 1)
                            wait(act, W.v_done, i * G)
                            shift_split(s1 * 2 + 1 if h == 0 else (s1 * 2 + 2) % B, 1 - h)
                    if s3 is not None:
                        feed(1)
                        if g == 1:
                            wait(act, W.fn_ready, fb + 1)
                            copy(f_hi[:], f_xc[:]).then_inc(W.fn_hi, 1)
                        elif g == 2:
                            gelu(0)
                            gelu(1)

            def reload_projection(layer):
                split_projection(layer + 1, (layer + 1) * (B * G))

            def reload_rest(layer):
                split_w1(layer + 1)
                act.wait_ge(W.vec_ready, layer + 2)

            schedule(act, body, reload_projection, reload_rest)
            act.wait_ge(W.f_free, DEPTH * B * FU + 1)
            with act.Fori(0, B) as b:
                wait(act, W.fin_tr, b + 1)
                copy(x_fin, X[:, b, 1:S + 1]).then_inc(W.fin_copy, 1)

        @block.gpsimd
        def _(pool):
            gp = nc.gpsimd
            for first in (W.f_free, W.a_av, W.a_av, W.y_tr, W.fin_add, W.fin_tr):
                pool.sem_inc(first, 1)
            gp.memset(X[:, :, 0:1], 0.0).then_inc(W.pool_zero, 1)
            gp.memset(qbd[:], 0.0).then_inc(W.pool_zero, 1)
            gp.memset(pt[:], 0.0).then_inc(W.pool_zero, 1)
            pool.wait_ge(W.pool_zero, 3)
            gp.memset(top[:], 0.0).then_inc(W.zeroed, 1)

            def body(n0, i0, s1, s3):
                for c in range(RING):
                    n, g, h = n0 + c, c % G, c // G
                    i = i0 + h
                    proj = live(n) and s1 is not None
                    fb = i - LAG_F

                    def add(s):
                        wait(pool, W.rot_done, n * 4 + 2 + 2 * s)
                        x = rotated[:, c, s, :, :]
                        gp.tensor_tensor(x, x, turned[:], ALU.add).then_inc(W.added, 1)

                    m = n - LAG_T
                    if live(m):
                        wait(pool, W.total_done, m + 1)
                        x = probs[:]
                        gp.tensor_tensor(x, x, total[:, 1, :].unsqueeze(2).to_broadcast([128, NW, 2 * WIN]),
                                         ALU.mult).then_inc(W.scaled, 1)
                    if proj:
                        add(0)
                        wait(pool, W.sq_done, n * 2 + 2)
                        gp.tensor_tensor(squares[:, :, 0, :], squares[:, :, 0, :], squares[:, :, 1, :], ALU.add
                                         ).then_inc(W.sq_summed, 1)
                    if proj:
                        add(1)
                    if s3 is not None and g == 1:
                        wait(pool, W.fn_hi, fb + 1)
                        gp.tensor_tensor(f_lo[:], f_xc[:], f_hi[:].bitcast(F32), ALU.subtract).then_inc(W.fn_lo, 1)

            pool.wait_ge(W.stats, 6)
            gp.memset(vring[0:WIN, :, 0, :], 0.0).then_inc(W.v_pad, 1)
            schedule(pool, body, lambda layer: None, lambda layer: None)


CLOADS = 11

_INS = ['L0_attn_x', 'L0_ffn_Wqkv', 'L0_ffn_Wo', 'L0_ffn_W1', 'L0_ffn_W2']


def lay_out(x):
    got = {"wqk_t": np.stack([np.asarray(x["L0_attn_w_q"]).T, np.asarray(x["L0_attn_w_k"]).T], 1),
           "bqk": np.stack([np.asarray(x["L0_attn_b_q"]), np.asarray(x["L0_attn_b_k"])], 1)}
    qks = [np.asarray(x[w]).reshape(DEPTH, 2, HALF).transpose(2, 0, 1) for w in ("L0_ffn_q_scale", "L0_ffn_k_scale")]
    got["qks"] = np.tile(np.concatenate(qks, 2), (HPG, 1, 1))
    vecs = np.zeros((128, DEPTH, 9), np.float32)
    for k, w in enumerate(("L0_ffn_ln_g", "L0_ffn_ln_b", "L0_ffn_b2")):
        vecs[:, :, k] = np.asarray(x[w]).T
    b1 = np.asarray(x["L0_ffn_b1"])
    for k, off in ((3, FF), (6, 0)):
        for c, m in enumerate(FCH):
            vecs[0:m, :, k + c] = b1[:, off + 128 * c:off + 128 * c + m].T
    got["vecs"] = vecs
    return {n: np.ascontiguousarray(v) for n, v in got.items()}


def kernel(**inputs):
    import numpy as _np
    import concourse.bacc as _bacc
    from concourse import mybir as _mybir
    from concourse.bass_utils import run_bass_kernel_spmd as _run

    nc = _bacc.Bacc("TRN2", target_bir_lowering=False, num_devices=1)
    values = {name: _np.ascontiguousarray(inputs[name]) for name in _INS}
    values.update(lay_out(inputs))
    values.update(constants())
    arrays, handles = {}, {}
    for name, value in values.items():
        arrays[f"in_{name}"] = value
        handles[name] = nc.dram_tensor(f"in_{name}", value.shape, _mybir.dt.from_np(value.dtype),
                                       kind="ExternalInput").ap()
    out = nc.dram_tensor("out_0", (B, S, D), F32, kind="ExternalOutput").ap()
    build(nc, handles, out)
    r = _run(nc, [arrays], core_ids=[0])
    return r.results[0]["out_0"]
```
